# Optimizing a Trainium2 kernel written in Bass

```python
import numpy as np
import jax
import jax.numpy as jnp

def _softmax(x, axis=-1):
    return jax.nn.softmax(x, axis=axis)

def _gelu(x):
    return jax.nn.gelu(x, approximate=True)

def _silu(x):
    return jax.nn.silu(x)

def _sigmoid(x):
    return jax.nn.sigmoid(x)

def _layernorm(x, axis=-1, eps=1e-05):
    m = jnp.mean(x, axis=axis, keepdims=True)
    v = jnp.var(x, axis=axis, keepdims=True)
    return (x - m) / jnp.sqrt(v + eps)

def _scatter_add(tgt, idx, src, axis=0):
    return tgt.at[idx].add(src)

def _segment_sum(src, seg, n):
    return jax.ops.segment_sum(src, seg, n)
kernel_name = 'mk_adaln_attn_ffn_d1_seqx_r8_8a01f5'

def setup_inputs(seed: int=0):
    np.random.seed(seed)
    _w = jnp.asarray

    def _rec_inputs():
        import jax
        import jax.numpy as jnp
        _rk = jax.random.key(seed)
        x = -7.109e-05 + 0.9999 * jax.random.normal(jax.random.fold_in(_rk, 1), (64, 32, 512), jnp.float32)
        _lenS = 32 - jax.random.randint(jax.random.fold_in(_rk, 7), (64,), 0, max(1, 32 // 4) + 1, jnp.int32)
        _lenS2 = 32 - jax.random.randint(jax.random.fold_in(_rk, 8), (64,), 0, max(1, 32 // 4) + 1, jnp.int32)
        itok_B_0_15 = jax.random.randint(jax.random.fold_in(_rk, 11), (64,), 0, 16, jnp.int32)
        itok_B_0_7 = jax.random.randint(jax.random.fold_in(_rk, 12), (64,), 0, 8, jnp.int32)
        return (x, itok_B_0_15, itok_B_0_7)
    x, itok_B_0_15, itok_B_0_7 = _rec_inputs()

    def _L0_cond_setup():
        import jax, jax.numpy as jnp
        import numpy as np
        B, C, T = (64, 32, 512)
        S, D = (16, 32)
        key = jax.random.key(seed)
        k1, k2, k3 = jax.random.split(key, 3)
        x = jax.random.normal(k1, (B, C, T), dtype=jnp.float32)
        condition = jax.random.randint(k2, (B,), 0, S, dtype=jnp.int64)
        bound = float(np.sqrt(6.0 / C))
        weights = jax.random.uniform(k3, (S, C, D), dtype=jnp.float32, minval=-bound, maxval=bound)
        return {'x': x, 'condition': condition, 'weights': weights}
    _L0_cond_all = _L0_cond_setup()
    _L0_cond_in = {k: v for k, v in _L0_cond_all.items() if k in ('weights',)}
    del _L0_cond_all

    def _L0_attn_setup():
        import jax, jax.numpy as jnp
        import numpy as np
        H = 32
        HKV = 8
        D = 512
        HD = D // H
        S = 128
        MASK_OUT = 0.9
        MIN_REMAIN = 128
        THETA = 10000.0

        def rope_tables(seq_len, hd):
            inv_freq = 1.0 / THETA ** (jnp.arange(0, hd, 2, dtype=jnp.float32) / hd)
            t = jnp.arange(seq_len, dtype=jnp.float32)
            freqs = jnp.outer(t, inv_freq)
            emb = jnp.concatenate([freqs, freqs], axis=-1)
            return (jnp.cos(emb), jnp.sin(emb))

        def rotate_half(x):
            x1, x2 = jnp.split(x, 2, axis=-1)
            return jnp.concatenate([-x2, x1], axis=-1)

        def apply_rope(x, cos, sin):
            return x * cos + rotate_half(x) * sin
        key = jax.random.key(seed)
        k0, k1, k2, k3, k4 = jax.random.split(key, 5)
        hidden_states = jax.random.normal(k0, (1, S, D), jnp.float32)
        Wq = jax.random.normal(k1, (D, D), jnp.float32) * 0.02
        Wk = jax.random.normal(k2, (HKV * HD, D), jnp.float32) * 0.02
        Wv = jax.random.normal(k3, (HKV * HD, D), jnp.float32) * 0.02
        Wo = jax.random.normal(k4, (D, D), jnp.float32) * 0.02
        return {'hidden_states': hidden_states, 'Wq': Wq, 'Wk': Wk, 'Wv': Wv, 'Wo': Wo}
    _L0_attn_all = _L0_attn_setup()
    _L0_attn_in = {k: v for k, v in _L0_attn_all.items() if k in ('Wq', 'Wk', 'Wv', 'Wo')}
    del _L0_attn_all

    def _L0_cond2_setup():
        import jax, jax.numpy as jnp
        import numpy as np
        TOP_K = 2
        LANG_BIAS = 5.0
        SCALING = 32.0 / 16.0
        LANGUAGE_PAD_ID = -1
        key = jax.random.key(seed)
        ks = jax.random.split(key, 6)
        B, T, D, O, E, R = (4, 256, 512, 512, 8, 16)
        x = jax.random.normal(ks[0], (B, T, D), dtype=jnp.float32)
        language_ids = jax.random.randint(ks[1], (B,), 0, E).astype(jnp.int64)
        W = jax.random.normal(ks[2], (O, D), dtype=jnp.float32) * (1.0 / np.sqrt(D))
        Wr = jax.random.normal(ks[3], (E, D), dtype=jnp.float32) * (1.0 / np.sqrt(D))
        A = jax.random.normal(ks[4], (E, R, D), dtype=jnp.float32) * (1.0 / np.sqrt(D))
        Bm = jax.random.normal(ks[5], (O, R), dtype=jnp.float32) * 0.0
        Bm = jnp.broadcast_to(Bm, (E, O, R)) + jax.random.normal(ks[5], (E, O, R), dtype=jnp.float32) * 0.02
        return {'x': x, 'language_ids': language_ids, 'W': W, 'Wr': Wr, 'A': A, 'B': Bm}
    _L0_cond2_all = _L0_cond2_setup()
    _L0_cond2_in = {k: v for k, v in _L0_cond2_all.items() if k in ('W', 'Wr', 'A', 'B')}
    del _L0_cond2_all

    def _L0_ffn_setup():
        import jax, jax.numpy as jnp
        import numpy as np
        key = jax.random.key(seed)
        k = jax.random.split(key, 6)
        x = jax.random.normal(k[0], (4, 256, 512), jnp.float32)
        W = jax.random.normal(k[1], (512, 512), jnp.float32) * 0.02
        bias = jax.random.normal(k[2], (512,), jnp.float32) * 0.02
        A = jax.random.normal(k[3], (16, 16, 512), jnp.float32) * 0.02
        Bf = jax.random.normal(k[4], (16, 512, 16), jnp.float32) * 0.02
        coeffs = jax.random.uniform(k[5], (16,), jnp.float32)
        scales = jnp.full((16,), 0.5, jnp.float32)
        return {'x': x, 'W': W, 'bias': bias, 'A': A, 'Bf': Bf, 'coeffs': coeffs, 'scales': scales}
    _L0_ffn_all = _L0_ffn_setup()
    _L0_ffn_in = {k: v for k, v in _L0_ffn_all.items() if k in ('W', 'bias', 'A', 'Bf', 'coeffs', 'scales')}
    del _L0_ffn_all
    return {'x': x, 'itok_B_0_15': itok_B_0_15, 'itok_B_0_7': itok_B_0_7, 'L0_cond_weights': _L0_cond_in['weights'], 'L0_attn_Wq': _L0_attn_in['Wq'], 'L0_attn_Wk': _L0_attn_in['Wk'], 'L0_attn_Wv': _L0_attn_in['Wv'], 'L0_attn_Wo': _L0_attn_in['Wo'], 'L0_cond2_W': _L0_cond2_in['W'], 'L0_cond2_Wr': _L0_cond2_in['Wr'], 'L0_cond2_A': _L0_cond2_in['A'], 'L0_cond2_B': _L0_cond2_in['B'], 'L0_ffn_W': _L0_ffn_in['W'], 'L0_ffn_bias': _L0_ffn_in['bias'], 'L0_ffn_A': _L0_ffn_in['A'], 'L0_ffn_Bf': _L0_ffn_in['Bf'], 'L0_ffn_coeffs': _L0_ffn_in['coeffs'], 'L0_ffn_scales': _L0_ffn_in['scales']}

def reference(x, itok_B_0_15, itok_B_0_7, L0_cond_weights, L0_attn_Wq, L0_attn_Wk, L0_attn_Wv, L0_attn_Wo, L0_cond2_W, L0_cond2_Wr, L0_cond2_A, L0_cond2_B, L0_ffn_W, L0_ffn_bias, L0_ffn_A, L0_ffn_Bf, L0_ffn_coeffs, L0_ffn_scales):
    import jax
    import jax.numpy as jnp

    def _L0_cond_ref(x, condition, weights):
        import jax, jax.numpy as jnp
        import numpy as np
        B, C, T = (64, 32, 512)
        S, D = (16, 32)
        W = weights[condition]
        return jnp.einsum('bct,bcd->bdt', x, W)

    def _L0_attn_ref(hidden_states, Wq, Wk, Wv, Wo):
        import jax, jax.numpy as jnp
        import numpy as np
        H = 32
        HKV = 8
        D = 512
        HD = D // H
        S = 128
        MASK_OUT = 0.9
        MIN_REMAIN = 128
        THETA = 10000.0

        def rope_tables(seq_len, hd):
            inv_freq = 1.0 / THETA ** (jnp.arange(0, hd, 2, dtype=jnp.float32) / hd)
            t = jnp.arange(seq_len, dtype=jnp.float32)
            freqs = jnp.outer(t, inv_freq)
            emb = jnp.concatenate([freqs, freqs], axis=-1)
            return (jnp.cos(emb), jnp.sin(emb))

        def rotate_half(x):
            x1, x2 = jnp.split(x, 2, axis=-1)
            return jnp.concatenate([-x2, x1], axis=-1)

        def apply_rope(x, cos, sin):
            return x * cos + rotate_half(x) * sin
        B, Sq, Dm = hidden_states.shape
        dtype = hidden_states.dtype
        neg = jnp.finfo(dtype).min
        q = (hidden_states @ Wq.T).reshape(B, Sq, H, HD).transpose(0, 2, 1, 3)
        k = (hidden_states @ Wk.T).reshape(B, Sq, HKV, HD).transpose(0, 2, 1, 3)
        v = (hidden_states @ Wv.T).reshape(B, Sq, HKV, HD).transpose(0, 2, 1, 3)
        rep = H // HKV
        k = jnp.repeat(k, rep, axis=1)
        v = jnp.repeat(v, rep, axis=1)
        cos, sin = rope_tables(Sq, HD)
        qr = apply_rope(q, cos, sin)
        kr = apply_rope(k, cos, sin)
        draft = jnp.einsum('bhqd,bhkd->bhqk', qr, kr)
        qi = jnp.arange(Sq)
        ki = jnp.arange(Sq)
        causal_future = qi[:, None] < ki[None, :]
        draft = draft + jnp.where(causal_future, neg, jnp.asarray(0.0, dtype))
        num_remain = max(min(Sq, MIN_REMAIN), Sq - int(Sq * MASK_OUT))
        _, draft_indices = jax.lax.top_k(draft, num_remain)
        mask = jnp.full((B, H, Sq, Sq), neg, dtype)
        b_idx = jnp.arange(B)[:, None, None, None]
        h_idx = jnp.arange(H)[None, :, None, None]
        s_idx = jnp.arange(Sq)[None, None, :, None]
        mask = mask.at[b_idx, h_idx, s_idx, draft_indices].set(0.0)
        mask = jnp.where(causal_future[None, None, :, :], neg, mask)
        scores = jnp.einsum('bhqd,bhkd->bhqk', qr, kr) / np.sqrt(HD).astype(np.float32) + mask
        attn = jax.nn.softmax(scores, axis=-1)
        out = jnp.einsum('bhqk,bhkd->bhqd', attn, v)
        out = out.transpose(0, 2, 1, 3).reshape(B, Sq, Dm)
        return out @ Wo.T

    def _L0_cond2_ref(x, language_ids, W, Wr, A, B):
        import jax, jax.numpy as jnp
        import numpy as np
        TOP_K = 2
        LANG_BIAS = 5.0
        SCALING = 32.0 / 16.0
        LANGUAGE_PAD_ID = -1
        base = jnp.einsum('btd,od->bto', x, W)
        E = Wr.shape[0]
        logits = jnp.einsum('btd,ed->bte', x.astype(jnp.float32), Wr.astype(jnp.float32))
        expert_targets = language_ids
        valid = expert_targets >= 0
        tgt = jnp.where(valid, expert_targets, 0)
        bias = jax.nn.one_hot(tgt, E, dtype=logits.dtype) * LANG_BIAS
        bias = jnp.where(valid[:, None], bias, 0.0)
        logits = logits + bias[:, None, :]
        topw, topi = jax.lax.top_k(logits, TOP_K)
        weights = jax.nn.softmax(topw, axis=-1)
        gates = jnp.sum(jax.nn.one_hot(topi, E, dtype=weights.dtype) * weights[..., None], axis=-2)
        gates = gates.astype(x.dtype)
        h = jnp.einsum('btd,erd->bter', x, A)
        lora_out = jnp.einsum('bter,bte,eor->bto', h, gates, B)
        return base + SCALING * lora_out

    def _L0_ffn_ref(x, W, bias, A, Bf, coeffs, scales):
        import jax, jax.numpy as jnp
        import numpy as np
        out = jnp.einsum('bsd,od->bso', x, W) + bias
        xa = jnp.einsum('bsd,erd->ebsr', x, A)
        w = coeffs * scales
        upd = jnp.einsum('ebsr,eor,e->bso', xa, Bf, w)
        return out + upd
    x = x + _L0_attn_ref(_L0_cond_ref(x, itok_B_0_15, L0_cond_weights), L0_attn_Wq, L0_attn_Wk, L0_attn_Wv, L0_attn_Wo)
    x = x + _L0_ffn_ref(_L0_cond2_ref(x, itok_B_0_7, L0_cond2_W, L0_cond2_Wr, L0_cond2_A, L0_cond2_B), L0_ffn_W, L0_ffn_bias, L0_ffn_A, L0_ffn_Bf, L0_ffn_coeffs, L0_ffn_scales)
    return x

_drawn_inputs = setup_inputs


def setup_inputs(seed=0):
    import zlib

    import numpy as np

    out = dict(_drawn_inputs(seed))
    spreads = {'L0_ffn_scales': (0.5, 0.6)}
    factors = {'L0_cond2_Wr': 8.0, 'L0_ffn_bias': 3.152, 'L0_ffn_coeffs': 3.455}
    for name, (base, spread) in spreads.items():
        noise = np.random.default_rng([zlib.crc32(name.encode()), seed]).standard_normal(out[name].shape)
        drawn = base * np.exp(spread * noise) if base else spread * noise
        out[name] = jnp.asarray(drawn.astype(out[name].dtype))
    for name, factor in factors.items():
        out[name] = (out[name] * factor).astype(out[name].dtype)
    return out
```

```python
from contextlib import ExitStack

import concourse.bass as bass
from concourse import mybir
import numpy as np

P = 128
NSEQ, S, D = 64, 32, 512
SEQ_PER_TILE = P // S
TILES = NSEQ // SEQ_PER_TILE
PAIRS = TILES // 2
SLOTS = 2 * SEQ_PER_TILE
HKV, REP, HD = 8, 4, 16
C = D // P
QKV = D + 2 * HKV * HD
E2, R2 = 8, 16
EF = 16
ROUT = E2 * R2 + E2
FW = ROUT + D
HALF = FW // 2
OUT_A = HALF - ROUT
LANG_BIAS = 5.0
SCALING = 2.0
MASKED = -1.0e30
GATE_STEPS = 13

F32 = mybir.dt.float32
F32R = mybir.dt.float32r
I32 = mybir.dt.int32
U32 = mybir.dt.uint32
ALU = mybir.AluOpType
ACT = mybir.ActivationFunctionType
AX = mybir.AxisListType

K_COS, K_SIN, K_MASK, K_IOTA, K_ID = 0, HD, 2 * HD, 2 * HD + S, 2 * HD + S + E2
K_ALL = K_ID + P

LOOP_FROM, LOOP_TO = 2, PAIRS - 2


def program(nc, x, xT, cond, lang, wcond, wqkv, wo, w2, a2r, b2, wf, af, bf, coeffs, scales, bias, consts, out):
    x_t = x.rearrange("(n b) c f -> n (b c) f", b=SEQ_PER_TILE)
    out_t = out.rearrange("(n b) c f -> n (b c) f", b=SEQ_PER_TILE)
    xT_p = xT.rearrange("(c p) n -> p c n", p=P)

    ctx = ExitStack()
    with ctx:
        def sb(name, shape, dt=F32):
            return ctx.enter_context(nc.sbuf_tensor(name, shape, dt))

        def pb(name, shape):
            return ctx.enter_context(nc.psum_tensor(name, shape, F32))

        def sem(name):
            return ctx.enter_context(nc.semaphore(name))

        def pair_of(name, shape):
            return sb(name + "_hi", shape, F32R), sb(name + "_lo", shape, F32R)

        const = sb("const", [P, K_ALL])
        cos = const[:, K_COS:K_COS + HD]
        sin = const[:, K_SIN:K_SIN + HD]
        mask = const[:, K_MASK:K_MASK + S]
        iota = const[:, K_IOTA:K_IOTA + E2]
        ident = const[:, K_ID:K_ID + P]
        cond_sb = sb("cond_sb", [1, NSEQ], I32)
        wqkv_raw = sb("wqkv_raw", [P, C, QKV])
        wqkv_hi, wqkv_lo = pair_of("wqkv", [P, C, QKV])
        wo_raw = sb("wo_raw", [P, C, D])
        wo_hi, wo_lo = pair_of("wo", [P, C, D])
        w2_sb = sb("w2_sb", [P, C, D])
        wf_sb = sb("wf_sb", [P, C, D])
        wfull = sb("wfull", [P, C, D])
        a2r_sb = sb("a2r_sb", [P, C, ROUT])
        b2_sb = sb("b2_sb", [P, C, E2 * R2])
        af_sb = sb("af_sb", [P, 2, D])
        bf_sb = sb("bf_sb", [P, 2, D])
        cw = sb("cw", [P, 3, 2])
        bias_sb = sb("bias_sb", [P, D])
        fused = sb("fused", [P, 2, D])
        fw_hi, fw_lo = pair_of("fw", [P, C, FW])
        bc_hi, bc_lo = pair_of("bc", [P, D])
        xt = sb("xt", [P, 2, D])
        wbd = sb("wbd", [P, 2, P])
        hT_hi, hT_lo = pair_of("hT", [P, 2, C, P])
        rope_cos = sb("rope_cos", [P, 5, P])
        rope_sin = sb("rope_sin", [P, 5, P])
        qk = sb("qk", [P, 5, P])
        vst = sb("vst", [P, 2, P])
        kst = sb("kst", [P, 2, P])
        QT = sb("QT", [P, 2, SEQ_PER_TILE, REP, S])
        Kbd = sb("Kbd", [P, 2, HKV, P])
        Vbd = sb("Vbd", [P, 2, SEQ_PER_TILE, 2, 64])
        v_dram = nc.dram_tensor("v_scratch", [2, P, P], F32).ap()
        att = sb("att", [P, 2, HKV, S])
        rowmax = sb("rowmax", [P, 2, HKV])
        rowsum = sb("rowsum", [P, 2, HKV])
        rowinv = sb("rowinv", [P, 2, HKV])
        PTs = sb("PTs", [P, 2, 2, P])
        oT_hi, oT_lo = pair_of("oT", [P, REP, 2, SEQ_PER_TILE, S])
        xres = sb("xres", [P, C, 2 * P])
        x1 = sb("x1", [P, C, 2 * P])
        x1_hi, x1_lo = pair_of("x1T", [P, C, 2 * P])
        ids = sb("ids", [P, 2], I32)
        lbias = sb("lbias", [P, E2])
        logits = sb("logits", [P, E2])
        top8 = sb("top8", [P, E2])
        idx8 = sb("idx8", [P, E2], U32)
        idxf = sb("idxf", [P, 2])
        gs = sb("gs", [P, 8])
        g_a = sb("g_a", [P, E2])
        gates = sb("gates", [P, E2])
        gh = sb("gh", [P, E2 * R2])
        ghT_hi, ghT_lo = pair_of("ghT", [P, P])
        y = sb("y", [P, 2, D])

        b_mix = pb("b_mix", [P, 512])
        b_qkv = pb("b_qkv", [P, 1024])
        b_out0 = pb("b_out0", [P, 512])
        b_out1 = pb("b_out1", [P, 512])
        b_s = pb("b_s", [P, 512])
        b_pt = pb("b_pt", [P, 512])
        b_o = pb("b_o", [P, 512])
        b_out = [b_out0, b_out1]

        names = """const_in cond_in wqkv_in wo_in prep_in bias_in zeroed wqkv_h wqkv_l wo_h wo_l
            scaled wprod wfull_sb fused_sb fused_h fused_l a2r_h a2r_l
            mixed hT_h hT_l q_done kv_done rope_terms roped v_out qT kT qT_sb kT_sb
            scored masked maxed shifted expd summed inverted normed pT pT_sb pv oT_h oT_l
            wo_done x1_sum x1_h x1_l fin gate_steps gate_exp gated ghT ghT_h ghT_l fin2 y_sb
            xres_in ids_in sp_passed"""
        sm = {n: sem(n) for n in names.split()}
        x_in = [sem(f"x_in{t}") for t in range(2)]
        w_in = [sem(f"w_in{t}") for t in range(2)]
        v_scr = [sem(f"v_scr{t}") for t in range(2)]
        v_in = [sem(f"v_in{t}") for t in range(2)]
        k_in = [sem(f"k_in{t}") for t in range(2)]
        stored = [sem(f"stored{t}") for t in range(2)]

        def steps(engine, body):
            for i in range(-2, LOOP_FROM):
                body(i, i)
            with engine.Fori(LOOP_FROM, LOOP_TO) as i:
                body(i, LOOP_FROM)
            for i in range(LOOP_TO, PAIRS + 2):
                body(i, i)

        def pair(k):
            return 0 <= k < PAIRS

        block = ctx.enter_context(nc.Block())

        @block.sync
        def _(sp):
            sp.dma_start(cond_sb[0:1, :], cond.rearrange("(a n) -> a n", a=1)).then_inc(sm["cond_in"], 16)
            sp.dma_start(const[:, :], consts).then_inc(sm["const_in"], 16)
            sp.wait_ge(sm["cond_in"], 16)
            sp.wait_ge(sm["zeroed"], 3)

            def settled():
                sp.wait_ge(sm["cond_in"], 16)

            def load_x(n, t):
                settled()
                sp.dma_start(xt[:, t, :], x_t[2 * n + t]).then_inc(x_in[t], 16)
                for b in range(SEQ_PER_TILE):
                    at = 8 * n + 4 * t + b
                    which = sp.value_load(cond_sb[0:1, bass.ds(at, 1)], min_val=0, max_val=15)
                    sp.dma_start(wbd[S * b:S * b + S, t, S * b:S * b + S],
                                 wcond[bass.ds(which, 1)].rearrange("a c d -> (a c) d")).then_inc(w_in[t], 16)

            def spread_v(t):
                src = v_dram[t].rearrange("(k b) (h g d) -> k (b h) g d", b=SEQ_PER_TILE, h=2, g=4)
                for g in range(4):
                    dst = Vbd[S * g:S * g + S, t, :, :, HD * g:HD * g + HD]
                    sp.dma_start(dst.rearrange("p b h d -> p (b h) d"), src[:, :, g, :]).then_inc(v_in[t], 16)

            def passed():
                sp.sem_inc(sm["sp_passed"], 1)

            def v_to_dram(n, k, t):
                sp.wait_ge(sm["v_out"], 2 * n + t + 1)
                if k > 0:
                    passed()
                    sp.wait_ge(v_in[t], 64 * n)
                sp.dma_start(v_dram[t].rearrange("(k b) c -> b k c", b=SEQ_PER_TILE),
                             vst[:, t, :]).then_inc(v_scr[t], 16)

            def spread_k(n, k, t):
                sp.wait_ge(sm["kT_sb"], 2 * n + t + 1)
                for g in range(HKV):
                    r = slice(HD * g, HD * g + HD)
                    sp.dma_start(Kbd[r, t, g, :], kst[r, t, :]).then_inc(k_in[t], 16)

            def body(i, k):
                if pair(k + 2):
                    if k > -2:
                        sp.wait_ge(sm["mixed"], 2 * (i + 1) + 1)
                    load_x(i + 2, 0)
                if pair(k):
                    sp.wait_ge(v_scr[1], 16 * (i + 1))
                    if k > 0:
                        passed()
                        sp.wait_ge(sm["pv"], 8 * i)
                    spread_v(1)
                if pair(k - 2):
                    sp.wait_ge(sm["y_sb"], 2 * (2 * (i - 2) + 2))
                    settled()
                    sp.dma_start(out_t[2 * (i - 2) + 1], y[:, 1, :]).then_inc(stored[1], 16)
                if pair(k - 1):
                    if k > 1:
                        sp.wait_ge(sm["gated"], 2 * (i - 2) + 2)
                    settled()
                    sp.dma_start(ids[:, :], lang[i - 1]).then_inc(sm["ids_in"], 16)
                if pair(k + 1):
                    v_to_dram(i + 1, k + 1, 0)
                if pair(k + 2):
                    if k > -2:
                        sp.wait_ge(sm["mixed"], 2 * (i + 1) + 2)
                    load_x(i + 2, 1)
                if pair(k + 1):
                    spread_k(i + 1, k + 1, 0)
                if pair(k):
                    if k > 0:
                        sp.wait_ge(sm["x1_sum"], 2 * (i - 1) + 2)
                    settled()
                    sp.dma_start(xres[:, :, :], xT_p[:, :, bass.ds(i * (2 * P), 2 * P)]).then_inc(sm["xres_in"], 16)
                if pair(k + 1):
                    sp.wait_ge(v_scr[0], 16 * (i + 2))
                    if k >= 0:
                        passed()
                        sp.wait_ge(sm["pv"], 8 * i + 4)
                    spread_v(0)
                    v_to_dram(i + 1, k + 1, 1)
                if pair(k - 1):
                    sp.wait_ge(sm["y_sb"], 2 * (2 * (i - 1) + 1))
                    settled()
                    sp.dma_start(out_t[2 * (i - 1)], y[:, 0, :]).then_inc(stored[0], 16)
                if pair(k + 1):
                    spread_k(i + 1, k + 1, 1)

            steps(sp, body)
            for t in range(2):
                sp.wait_ge(stored[t], 16 * PAIRS)
                sp.wait_ge(v_scr[t], 16 * PAIRS)

        @block.gpsimd
        def _(pool):
            nc.gpsimd.memset(wbd[:, :, :], 0.0).then_inc(sm["zeroed"], 1)
            nc.gpsimd.memset(Kbd[:, :, :, :], 0.0).then_inc(sm["zeroed"], 1)
            nc.gpsimd.memset(Vbd[:, :, :, :, :], 0.0).then_inc(sm["zeroed"], 1)

            def subtract(dst, full, high, signal):
                nc.gpsimd.tensor_tensor(dst, full, high.bitcast(F32), ALU.subtract).then_inc(signal, 1)

            def shift(i, s):
                pool.wait_ge(sm["maxed"], 8 * i + s + 1)
                m = rowmax[:, s % 2, :].unsqueeze(2).broadcast_to([P, HKV, S])
                nc.gpsimd.tensor_tensor(att[:, s % 2], att[:, s % 2], m, ALU.subtract).then_inc(sm["shifted"], 1)

            def normalise(i, s):
                pool.wait_ge(sm["inverted"], 8 * i + s + 1)
                r = rowinv[:, s % 2, :].unsqueeze(2).broadcast_to([P, HKV, S])
                nc.gpsimd.tensor_tensor(att[:, s % 2], att[:, s % 2], r, ALU.mult).then_inc(sm["normed"], 1)

            def rope_sum(n, t):
                pool.wait_ge(sm["rope_terms"], 3 * (2 * n + t) + 3)
                nc.gpsimd.tensor_tensor(qk[:, :, :], rope_cos[:, :, :], rope_sin[:, :, :],
                                        ALU.add).then_inc(sm["roped"], 1)

            def x1_low(p, h):
                pool.wait_ge(sm["x1_h"], 2 * p + h + 1)
                subtract(x1_lo[:, 2 * h:2 * h + 2, :], x1[:, 2 * h:2 * h + 2, :],
                         x1_hi[:, 2 * h:2 * h + 2, :], sm["x1_l"])

            def fused_low(m):
                pool.wait_ge(sm["fused_h"], m + 1)
                if m < C:
                    subtract(fw_lo[:, m, ROUT:FW], fused[:, m % 2, :], fw_hi[:, m, ROUT:FW], sm["fused_l"])
                else:
                    subtract(bc_lo[:, :], fused[:, m % 2, :], bc_hi[:, :], sm["fused_l"])

            def body(i, k):
                for s in range(SLOTS):
                    if pair(k):
                        shift(i, s)
                        normalise(i, s)
                    if s == 1 and pair(k + 1):
                        rope_sum(i + 1, 0)
                    if s in (2, 3) and pair(k - 1):
                        x1_low(i - 1, s - 2)
                    if s == 6 and pair(k + 1):
                        rope_sum(i + 1, 1)
                    if k == 0 and s == 0:
                        pool.wait_ge(sm["wo_h"], 1)
                        subtract(wo_lo[:, :, :], wo_raw[:, :, :], wo_hi[:, :, :], sm["wo_l"])
                        pool.wait_ge(sm["a2r_h"], 1)
                        subtract(fw_lo[:, :, 0:ROUT], a2r_sb[:, :, :], fw_hi[:, :, 0:ROUT], sm["a2r_l"])
                    if k == 0 and 4 <= s:
                        fused_low(s - 4)
                if k == 0:
                    fused_low(C)

            steps(pool, body)

        @block.scalar
        def _(act):
            act.dma_start(wqkv_raw[:, 0:2, :], wqkv[:, 0:2, :]).then_inc(sm["wqkv_in"], 16)
            act.dma_start(wqkv_raw[:, 2:4, :], wqkv[:, 2:4, :]).then_inc(sm["wqkv_in"], 16)
            act.dma_start(wo_raw[:, :, :], wo).then_inc(sm["wo_in"], 16)
            for dst, src in ((af_sb[:, :, :], af), (bf_sb[:, :, :], bf), (wf_sb[:, :, :], wf),
                             (w2_sb[:, :, :], w2), (b2_sb[:, :, :], b2), (a2r_sb[:, :, :], a2r),
                             (cw[:, 0, :], coeffs), (cw[:, 1, :], scales)):
                act.dma_start(dst, src).then_inc(sm["prep_in"], 16)
            act.dma_start(bias_sb[:, :], bias.rearrange("(a n) -> a n", a=1).broadcast_to([P, D])
                          ).then_inc(sm["bias_in"], 16)
            act.wait_ge(sm["wqkv_in"], 32)
            for c in range(C):
                nc.scalar.copy(wqkv_hi[:, c, :], wqkv_raw[:, c, :]).then_inc(sm["wqkv_h"], 1)

            def mix_high(n, t):
                act.wait_ge(sm["mixed"], 2 * n + t + 1)
                nc.scalar.copy(hT_hi[:, t].rearrange("p c n -> p (c n)"), b_mix[:, :]).then_inc(sm["hT_h"], 1)

            def value_copy(n, k, t):
                act.wait_ge(sm["kv_done"], 2 * n + t + 1)
                if k > 0:
                    act.wait_ge(v_scr[t], 16 * n)
                nc.scalar.copy(vst[:, t, :], b_qkv[:, D + P:D + 2 * P]).then_inc(sm["v_out"], 1)

            def qk_copy(n, k, t):
                act.wait_ge(sm["qT"], 2 * n + t + 1)
                src = b_qkv[:, 0:D].rearrange("p (r b s) -> p b r s", r=REP, b=SEQ_PER_TILE)
                nc.scalar.copy(QT[:, t], src).then_inc(sm["qT_sb"], 1)
                act.wait_ge(sm["kT"], 2 * n + t + 1)
                if k > 0:
                    act.wait_ge(k_in[t], 128 * n)
                nc.scalar.copy(kst[:, t, :], b_qkv[:, D:D + P]).then_inc(sm["kT_sb"], 1)

            def probs_T_copy(i, k, s):
                act.wait_ge(sm["pT"], 8 * i + s + 1)
                if k > 0 or s >= 2:
                    act.wait_ge(sm["pv"], 8 * i + s - 1)
                nc.scalar.copy(PTs[:, s % 2].rearrange("p h n -> p (h n)"), b_pt[:, 0:2 * P]).then_inc(sm["pT_sb"], 1)

            def exps(i, s):
                act.wait_ge(sm["shifted"], 8 * i + s + 1)
                nc.scalar.activation(att[:, s % 2], att[:, s % 2], ACT.Exp,
                                     scale=float(HD) ** -0.5).then_inc(sm["expd"], 1)

            def o_high(i, t):
                act.wait_ge(sm["pv"], 8 * i + 4 * t + 4)
                src = b_o[:, :].rearrange("p (b r s) -> p r b s", b=SEQ_PER_TILE, r=REP)
                nc.scalar.copy(oT_hi[:, :, t], src).then_inc(sm["oT_h"], 1)

            def x1_high(p, h):
                act.wait_ge(sm["x1_sum"], 2 * p + h + 1)
                nc.scalar.copy(x1_hi[:, 2 * h:2 * h + 2, :], x1[:, 2 * h:2 * h + 2, :]).then_inc(sm["x1_h"], 1)

            def gate_exp(p, t):
                act.wait_ge(sm["gate_steps"], GATE_STEPS * (2 * p + t) + 4)
                nc.scalar.activation(gs[:, 1:2], gs[:, 0:1], ACT.Exp).then_inc(sm["gate_exp"], 1)

            def gh_high(p, t):
                act.wait_ge(sm["ghT"], 2 * p + t + 1)
                nc.scalar.copy(ghT_hi[:, :], b_mix[:, 0:P]).then_inc(sm["ghT_h"], 1)

            def fused_high(m):
                act.wait_ge(sm["fused_sb"], 2 * m + 2 if m < C else 2 * C + 1)
                dst = fw_hi[:, m, ROUT:FW] if m < C else bc_hi[:, :]
                nc.scalar.copy(dst, fused[:, m % 2, :]).then_inc(sm["fused_h"], 1)

            def body(i, k):
                if pair(k - 2):
                    gate_exp(i - 2, 1)
                for s in range(SLOTS):
                    if s == 0:
                        if pair(k - 1):
                            probs_T_copy(i - 1, k - 1, SLOTS - 1)
                    elif pair(k):
                        probs_T_copy(i, k, s - 1)
                    if pair(k):
                        exps(i, s)
                    if s == 0 and pair(k - 2):
                        gh_high(i - 2, 1)
                    if s == 0 and pair(k - 1):
                        o_high(i - 1, 1)
                    if s == 0 and k == 0:
                        act.wait_ge(sm["wo_in"], 16)
                        nc.scalar.copy(wo_hi[:, :, :], wo_raw[:, :, :]).then_inc(sm["wo_h"], 1)
                        act.wait_ge(sm["prep_in"], 16 * 8)
                        nc.scalar.copy(fw_hi[:, :, 0:ROUT], a2r_sb[:, :, :]).then_inc(sm["a2r_h"], 1)
                    if s == 1 and pair(k + 1):
                        value_copy(i + 1, k + 1, 0)
                        mix_high(i + 1, 1)
                    if s in (2, 3) and pair(k - 1):
                        x1_high(i - 1, s - 2)
                    if s == 3 and pair(k + 1):
                        qk_copy(i + 1, k + 1, 0)
                    if s == 5 and pair(k):
                        o_high(i, 0)
                    if s == 5 and pair(k - 1):
                        gate_exp(i - 1, 0)
                    if s == 6:
                        if pair(k + 1):
                            value_copy(i + 1, k + 1, 1)
                        if pair(k - 1):
                            gh_high(i - 1, 0)
                        if pair(k + 2):
                            mix_high(i + 2, 0)
                    if s == 7 and pair(k + 1):
                        qk_copy(i + 1, k + 1, 1)
                    if k == 0 and 4 <= s:
                        fused_high(s - 4)
                if k == 0:
                    fused_high(C)

            steps(act, body)

        @block.vector
        def _(dve):
            def low(dst, full, high, signal):
                nc.vector.tensor_tensor(dst, full, high.bitcast(F32), ALU.subtract).then_inc(signal, 1)

            def mix_low(n, t):
                dve.wait_ge(sm["hT_h"], 2 * n + t + 1)
                low(hT_lo[:, t].rearrange("p c n -> p (c n)"), b_mix[:, :],
                    hT_hi[:, t].rearrange("p c n -> p (c n)"), sm["hT_l"])

            def rope_products(n, k, t):
                dve.wait_ge(sm["q_done"], 2 * n + t + 1)
                dve.wait_ge(sm["v_out"], 2 * n + t + 1)
                if k > 0 or t > 0:
                    dve.wait_ge(sm["roped"], 2 * n + t)
                heads = (D + P) // HD
                q = b_qkv[:, 0:D + P].rearrange("p (h d) -> p h d", d=HD)
                c_out = rope_cos[:, :, :].rearrange("p c (h d) -> p (c h) d", d=HD)
                s_out = rope_sin[:, :, :].rearrange("p c (h d) -> p (c h) d", d=HD)
                half = HD // 2
                nc.vector.tensor_tensor(c_out, q, cos.unsqueeze(1).broadcast_to([P, heads, HD]),
                                        ALU.mult).then_inc(sm["rope_terms"], 1)
                for lo, hi in ((0, half), (half, 0)):
                    nc.vector.tensor_tensor(s_out[:, :, lo:lo + half], q[:, :, hi:hi + half],
                                            sin[:, lo:lo + half].unsqueeze(1).broadcast_to([P, heads, half]),
                                            ALU.mult).then_inc(sm["rope_terms"], 1)

            def mask_and_max(i, k, s):
                dve.wait_ge(sm["scored"], 8 * i + s + 1)
                m = mask.unsqueeze(1).broadcast_to([P, HKV, S])
                nc.vector.tensor_tensor(att[:, s % 2], b_s[:, 0:HKV * S].rearrange("p (g k) -> p g k", g=HKV), m,
                                        ALU.add).then_inc(sm["masked"], 1)
                dve.wait_ge(sm["masked"], 8 * i + s + 1)
                nc.vector.tensor_reduce(rowmax[:, s % 2, :], att[:, s % 2], AX.X, ALU.max).then_inc(sm["maxed"], 1)

            def row_sums(i, s):
                dve.wait_ge(sm["expd"], 8 * i + s + 1)
                nc.vector.tensor_reduce(rowsum[:, s % 2, :], att[:, s % 2], AX.X, ALU.add).then_inc(sm["summed"], 1)
                dve.wait_ge(sm["summed"], 8 * i + s + 1)
                nc.vector.reciprocal(rowinv[:, s % 2, :], rowsum[:, s % 2, :]).then_inc(sm["inverted"], 1)

            def o_low(i, t):
                dve.wait_ge(sm["oT_h"], 2 * i + t + 1)
                src = b_o[:, :].rearrange("p (b r s) -> p r b s", b=SEQ_PER_TILE, r=REP)
                low(oT_lo[:, :, t], src, oT_hi[:, :, t], sm["oT_l"])

            def add_residual(p, h):
                dve.wait_ge(sm["wo_done"], 2 * p + h + 1)
                dve.wait_ge(sm["xres_in"], 16 * (p + 1))
                nc.vector.tensor_tensor(x1[:, 2 * h:2 * h + 2, :], b_out[h][:, :].rearrange("p (c n) -> p c n", c=2),
                                        xres[:, 2 * h:2 * h + 2, :], ALU.add).then_inc(sm["x1_sum"], 1)

            def gating(p, t):
                done = [GATE_STEPS * (2 * p + t)]

                def step(instruction):
                    done[0] = done[0] + 1
                    instruction.then_inc(sm["gate_steps"], 1)
                    dve.wait_ge(sm["gate_steps"], done[0])

                dve.wait_ge(sm["ids_in"], 16 * (p + 1))
                step(nc.vector.tensor_scalar(lbias[:, :], iota, ids[:, t:t + 1], LANG_BIAS, ALU.is_equal, ALU.mult))
                dve.wait_ge(sm["fin"], 2 * p + t + 1)
                step(nc.vector.tensor_tensor(logits[:, :], b_out0[:, E2 * R2:ROUT], lbias[:, :], ALU.add))
                nc.vector.tensor_copy(gs[:, 6:7], logits[:, 0:1])
                step(nc.vector.max(top8[:, :], logits[:, :]))
                nc.vector.tensor_tensor(gs[:, 0:1], top8[:, 1:2], top8[:, 0:1],
                                        ALU.subtract).then_inc(sm["gate_steps"], 1)
                done[0] = done[0] + 1
                step(nc.vector.max_index(idx8[:, :], top8[:, :], logits[:, :]))
                step(nc.vector.tensor_copy(idxf[:, :], idx8[:, 0:2]))
                dve.wait_ge(sm["gate_exp"], 2 * p + t + 1)
                step(nc.vector.tensor_scalar(gs[:, 2:3], gs[:, 1:2], 1.0, None, ALU.add))
                step(nc.vector.reciprocal(gs[:, 3:4], gs[:, 2:3]))
                nc.vector.tensor_scalar(gs[:, 4:5], gs[:, 3:4], SCALING, None, ALU.mult).then_inc(sm["gate_steps"], 1)
                done[0] = done[0] + 1
                step(nc.vector.tensor_scalar(gs[:, 5:6], gs[:, 3:4], gs[:, 1:2], SCALING, ALU.mult, ALU.mult))
                nc.vector.tensor_scalar(g_a[:, :], iota, idxf[:, 0:1], gs[:, 4:5], ALU.is_equal,
                                        ALU.mult).then_inc(sm["gate_steps"], 1)
                done[0] = done[0] + 1
                step(nc.vector.tensor_scalar(top8[:, :], iota, idxf[:, 1:2], gs[:, 5:6], ALU.is_equal, ALU.mult))
                step(nc.vector.tensor_tensor(gates[:, :], g_a[:, :], top8[:, :], ALU.add))
                nc.vector.tensor_tensor(gh[:, :].rearrange("p (e r) -> p e r", e=E2),
                                        b_out0[:, 0:E2 * R2].rearrange("p (e r) -> p e r", e=E2),
                                        gates[:, :].unsqueeze(2).broadcast_to([P, E2, R2]),
                                        ALU.mult).then_inc(sm["gated"], 1)

            def gh_low(p, t):
                dve.wait_ge(sm["ghT_h"], 2 * p + t + 1)
                low(ghT_lo[:, :], b_mix[:, 0:P], ghT_hi[:, :], sm["ghT_l"])

            def finish(p, k, t):
                dve.wait_ge(sm["fin2"], 2 * p + t + 1)
                if k > 0:
                    dve.wait_ge(stored[t], 16 * p)
                nc.vector.tensor_tensor(y[:, t, 0:OUT_A], b_out0[:, ROUT:HALF], bias_sb[:, 0:OUT_A],
                                        ALU.add).then_inc(sm["y_sb"], 1)
                nc.vector.tensor_tensor(y[:, t, OUT_A:D], b_out1[:, 0:HALF], bias_sb[:, OUT_A:D],
                                        ALU.add).then_inc(sm["y_sb"], 1)

            def full_weight(m):
                dve.wait_ge(sm["wprod"], m + 1)
                nc.vector.tensor_tensor(wfull[:, m, :], b_out[m % 2][:, :], wf_sb[:, m, :],
                                        ALU.add).then_inc(sm["wfull_sb"], 1)

            def fused_weight(m):
                dve.wait_ge(sm["wprod"], C + m + 1)
                if m >= 2:
                    dve.wait_ge(sm["fused_l"], m - 1)
                nc.vector.tensor_copy(fused[:, m % 2, :], b_out[m % 2][:, :]).then_inc(sm["fused_sb"], 1)
                if m < C:
                    dve.wait_ge(sm["fused_sb"], 2 * m + 1)
                    block_m = fused[:, m % 2, P * m:P * m + P]
                    nc.vector.tensor_tensor(block_m, block_m, ident, ALU.add).then_inc(sm["fused_sb"], 1)

            def body(i, k):
                if pair(k - 2):
                    gating(i - 2, 1)
                for s in range(SLOTS):
                    if s == 1 and pair(k - 2):
                        finish(i - 2, k - 2, 1)
                    if pair(k):
                        mask_and_max(i, k, s)
                    if s == 0 and pair(k - 2):
                        gh_low(i - 2, 1)
                    if s == 0 and pair(k - 1):
                        o_low(i - 1, 1)
                    if s == 6 and pair(k - 1):
                        gh_low(i - 1, 0)
                    if pair(k):
                        row_sums(i, s)
                    if s in (2, 3) and pair(k - 1):
                        add_residual(i - 1, s - 2)
                    if s == 1 and pair(k + 1):
                        rope_products(i + 1, k + 1, 0)
                        mix_low(i + 1, 1)
                    if s == 5 and pair(k):
                        o_low(i, 0)
                    if s == 5 and pair(k - 1):
                        gating(i - 1, 0)
                    if s == 6:
                        if pair(k + 1):
                            rope_products(i + 1, k + 1, 1)
                        if pair(k - 1):
                            finish(i - 1, k - 1, 0)
                        if pair(k + 2):
                            mix_low(i + 2, 0)
                    if k == 0 and s == 0:
                        dve.wait_ge(sm["prep_in"], 16 * 8)
                        nc.vector.tensor_tensor(cw[:, 2, :], cw[:, 0, :], cw[:, 1, :], ALU.mult).then_inc(sm["scaled"], 1)
                        dve.wait_ge(sm["scaled"], 1)
                        for e in range(2):
                            nc.vector.tensor_scalar(bf_sb[:, e, :], bf_sb[:, e, :], cw[:, 2, e:e + 1], None,
                                                    ALU.mult).then_inc(sm["scaled"], 1)
                    if k == 0 and s in (1, 2):
                        full_weight(2 * s - 2)
                        full_weight(2 * s - 1)
                    if k == 0 and s == 3:
                        fused_weight(0)
                    if k == 0 and s >= 4:
                        fused_weight(s - 3)
                if k == 0:
                    pass

            dve.wait_ge(sm["const_in"], 16)
            dve.wait_ge(sm["bias_in"], 16)
            for c in range(C):
                dve.wait_ge(sm["wqkv_h"], c + 1)
                low(wqkv_lo[:, c, :], wqkv_raw[:, c, :], wqkv_hi[:, c, :], sm["wqkv_l"])
            steps(dve, body)

        @block.tensor
        def _(pe):
            def split_product(dst, chunks):
                for c, (sh, sl, mh, ml) in enumerate(chunks):
                    for n, (a, b) in enumerate(((sh, mh), (sh, ml), (sl, mh))):
                        last = nc.tensor.matmul(dst, a, b, start=(c == 0 and n == 0),
                                                stop=(c == len(chunks) - 1 and n == 2))
                return last

            def mix(n, t):
                pe.wait_ge(x_in[t], 16 * (n + 1))
                pe.wait_ge(w_in[t], 64 * (n + 1))
                for c in range(C):
                    last = nc.tensor.matmul(b_mix[:, P * c:P * c + P], xt[:, t, P * c:P * c + P], wbd[:, t, :],
                                            start=True, stop=True)
                last.then_inc(sm["mixed"], 1)

            def project_q(n, k, t):
                pe.wait_ge(sm["hT_l"], 2 * n + t + 1)
                if k > 0 or t > 0:
                    pe.wait_ge(sm["qT_sb"], 2 * n + t)
                split_product(b_qkv[:, 0:D], [(hT_hi[:, t, c], hT_lo[:, t, c], wqkv_hi[:, c, 0:D], wqkv_lo[:, c, 0:D])
                                              for c in range(C)]).then_inc(sm["q_done"], 1)

            def project_kv(n, k, t):
                if k > 0 or t > 0:
                    pe.wait_ge(sm["kT_sb"], 2 * n + t)
                split_product(b_qkv[:, D:QKV], [(hT_hi[:, t, c], hT_lo[:, t, c], wqkv_hi[:, c, D:QKV],
                                                 wqkv_lo[:, c, D:QKV]) for c in range(C)]).then_inc(sm["kv_done"], 1)

            def transpose_qk(n, t):
                pe.wait_ge(sm["roped"], 2 * n + t + 1)
                for r in range(REP):
                    last = nc.tensor.transpose(b_qkv[:, P * r:P * r + P], qk[:, r, :], ident)
                last.then_inc(sm["qT"], 1)
                pe.wait_ge(sm["v_out"], 2 * n + t + 1)
                nc.tensor.transpose(b_qkv[:, D:D + P], qk[:, REP, :], ident).then_inc(sm["kT"], 1)

            def scores(i, k, s):
                t, b = s // SEQ_PER_TILE, s % SEQ_PER_TILE
                if b == 0:
                    pe.wait_ge(k_in[t], 128 * (i + 1))
                    pe.wait_ge(sm["qT_sb"], 2 * i + t + 1)
                if k > 0 or s > 0:
                    pe.wait_ge(sm["masked"], 8 * i + s)
                nc.tensor.matmul(b_s[:, 0:HKV * S], QT[:, t, b].rearrange("p r s -> p (r s)"),
                                 Kbd[:, t, :, S * b:S * b + S], start=True, stop=True).then_inc(sm["scored"], 1)

            def probs_T(i, k, s):
                pe.wait_ge(sm["normed"], 8 * i + s + 1)
                if k > 0 or s > 0:
                    pe.wait_ge(sm["pT_sb"], 8 * i + s)
                for h in range(2):
                    last = nc.tensor.transpose(b_pt[:, P * h:P * h + P],
                                               att[:, s % 2, 4 * h:4 * h + 4].rearrange("p g k -> p (g k)"), ident)
                last.then_inc(sm["pT"], 1)

            def values(i, k, s):
                t, b = s // SEQ_PER_TILE, s % SEQ_PER_TILE
                pe.wait_ge(sm["pT_sb"], 8 * i + s + 1)
                if b == 0:
                    pe.wait_ge(v_in[t], 64 * (i + 1))
                    if k > 0 or t > 0:
                        pe.wait_ge(sm["oT_l"], 2 * i + t)
                for h in range(2):
                    last = nc.tensor.matmul(b_o[64 * h:64 * h + 64, P * b:P * b + P], Vbd[:, t, b, h, :],
                                            PTs[:, s % 2, h, :], start=True, stop=True)
                last.then_inc(sm["pv"], 1)

            def output_projection(p, k, h):
                if h == 0:
                    if k > 0:
                        pe.wait_ge(sm["y_sb"], 4 * p)
                    else:
                        pe.wait_ge(sm["fused_sb"], 2 * C + 1)
                        pe.wait_ge(sm["wo_l"], 1)
                    pe.wait_ge(sm["oT_l"], 2 * p + 2)
                for c in (2 * h, 2 * h + 1):
                    o = [(wo_hi[:, r, P * c:P * c + P], wo_lo[:, r, P * c:P * c + P],
                          oT_hi[:, r].rearrange("p t b s -> p (t b s)"), oT_lo[:, r].rearrange("p t b s -> p (t b s)"))
                         for r in range(REP)]
                    last = split_product(b_out[h][:, 256 * (c % 2):256 * (c % 2) + 256], o)
                last.then_inc(sm["wo_done"], 1)

            def output_layers(p, k, t, part):
                if part == 0 and t == 0:
                    pe.wait_ge(sm["x1_l"], 2 * p + 2)
                    if k == 0:
                        pe.wait_ge(sm["fused_l"], C + 1)
                        pe.wait_ge(sm["a2r_l"], 1)
                if part == 0 and t == 1:
                    pe.wait_ge(sm["y_sb"], 2 * (2 * p + 1))
                for c in (2 * part, 2 * part + 1):
                    tok = slice(P * t, P * t + P)
                    for n, (a, b) in enumerate(((x1_hi, fw_hi), (x1_hi, fw_lo), (x1_lo, fw_hi))):
                        for h in range(2):
                            last = nc.tensor.matmul(b_out[h][:, 0:HALF], a[:, c, tok], b[:, c, HALF * h:HALF * h + HALF],
                                                    start=(c == 0 and n == 0), stop=(c == C - 1 and n == 2))
                if part == 1:
                    last.then_inc(sm["fin"], 1)

            def transpose_gated(p, t):
                pe.wait_ge(sm["gated"], 2 * p + t + 1)
                nc.tensor.transpose(b_mix[:, 0:P], gh[:, :], ident).then_inc(sm["ghT"], 1)

            def add_experts(p, t):
                pe.wait_ge(sm["ghT_l"], 2 * p + t + 1)
                for n, (a, b) in enumerate(((ghT_hi, bc_hi), (ghT_hi, bc_lo), (ghT_lo, bc_hi))):
                    nc.tensor.matmul(b_out0[:, ROUT:HALF], a[:, :], b[:, 0:OUT_A], start=False, stop=(n == 2),
                                     skip_group_check=True)
                    last = nc.tensor.matmul(b_out1[:, 0:HALF], a[:, :], b[:, OUT_A:D], start=False, stop=(n == 2),
                                            skip_group_check=True)
                last.then_inc(sm["fin2"], 1)

            def update_product(m):
                if m == 0:
                    pe.wait_ge(sm["prep_in"], 16 * 8)
                    pe.wait_ge(sm["scaled"], 3)
                if m >= 2:
                    pe.wait_ge(sm["wfull_sb"], m - 1)
                for e in range(2):
                    last = nc.tensor.matmul(b_out[m % 2][:, :], af_sb[:, e, P * m:P * m + P], bf_sb[:, e, :],
                                            start=(e == 0), stop=(e == 1))
                last.then_inc(sm["wprod"], 1)

            def fused_product(m):
                pe.wait_ge(sm["wfull_sb"], C)
                if m >= 2:
                    pe.wait_ge(sm["fused_sb"], 2 * (m - 2) + 1)
                for c in range(C):
                    left = w2_sb[:, c, P * m:P * m + P] if m < C else b2_sb[:, c, :]
                    last = nc.tensor.matmul(b_out[m % 2][:, :], left, wfull[:, c, :], start=(c == 0), stop=(c == C - 1))
                last.then_inc(sm["wprod"], 1)

            def body(i, k):
                a_next, a_after, w_now, w_tail = pair(k + 1), pair(k + 2), pair(k - 1), pair(k - 2)
                for s in range(SLOTS):
                    if pair(k):
                        scores(i, k, s)
                    if s == 0:
                        if w_now:
                            probs_T(i - 1, k - 1, SLOTS - 1)
                        if w_tail:
                            transpose_gated(i - 2, 1)
                        if a_next:
                            project_q(i + 1, k + 1, 0)
                        if w_now:
                            values(i - 1, k - 1, SLOTS - 1)
                        if a_next:
                            project_kv(i + 1, k + 1, 0)
                        if w_tail:
                            add_experts(i - 2, 1)
                        continue
                    if pair(k):
                        probs_T(i, k, s - 1)
                    if s == 1:
                        if a_next:
                            if w_tail:
                                pe.wait_ge(sm["ghT_l"], 2 * (i - 2) + 2)
                            mix(i + 1, 1)
                        if w_now:
                            output_projection(i - 1, k - 1, 0)
                        if k == 0:
                            update_product(0)
                            update_product(1)
                    if s == 2:
                        if w_now:
                            output_projection(i - 1, k - 1, 1)
                        if k == 0:
                            update_product(2)
                            update_product(3)
                    if s == 3:
                        if a_next:
                            transpose_qk(i + 1, 0)
                        if w_now:
                            output_layers(i - 1, k - 1, 0, 0)
                        if k == 0:
                            fused_product(0)
                    if s == 4:
                        if a_next:
                            project_q(i + 1, k + 1, 1)
                        if k == 0:
                            fused_product(1)
                    if s == 5:
                        if w_now:
                            output_layers(i - 1, k - 1, 0, 1)
                        if a_next:
                            project_kv(i + 1, k + 1, 1)
                        if k == 0:
                            fused_product(2)
                    if s == 6 and w_now:
                        transpose_gated(i - 1, 0)
                    if s == 7:
                        if a_next:
                            transpose_qk(i + 1, 1)
                        if w_now:
                            output_layers(i - 1, k - 1, 1, 0)
                            output_layers(i - 1, k - 1, 1, 1)
                        if k == 0:
                            fused_product(4)
                    if pair(k):
                        values(i, k, s - 1)
                    if s == 6:
                        if w_now:
                            add_experts(i - 1, 0)
                        if a_after:
                            mix(i + 2, 0)
                        if k == 0:
                            fused_product(3)

            pe.wait_ge(sm["const_in"], 16)
            pe.wait_ge(sm["wqkv_l"], C)
            steps(pe, body)


_OUT = (NSEQ, S, D)


def kernel(x, itok_B_0_15, itok_B_0_7, L0_cond_weights, L0_attn_Wq, L0_attn_Wk, L0_attn_Wv, L0_attn_Wo,
           L0_cond2_W, L0_cond2_Wr, L0_cond2_A, L0_cond2_B, L0_ffn_W, L0_ffn_bias, L0_ffn_A, L0_ffn_Bf,
           L0_ffn_coeffs, L0_ffn_scales):
    import concourse.bacc as _bacc
    from concourse.bass_utils import run_bass_kernel_spmd as _run

    def chunked(w, n=C):
        return np.ascontiguousarray(np.asarray(w).reshape(n, P, -1).transpose(1, 0, 2))

    x = np.ascontiguousarray(x)
    q_rows = np.asarray(L0_attn_Wq).reshape(HKV, REP, HD, D).transpose(1, 0, 2, 3).reshape(D, D)
    qkv_rows = np.concatenate([q_rows, np.asarray(L0_attn_Wk), np.asarray(L0_attn_Wv)], 0)
    o_cols = np.asarray(L0_attn_Wo).reshape(D, HKV, REP, HD).transpose(2, 1, 3, 0).reshape(D, D)
    a2 = np.asarray(L0_cond2_A).reshape(E2 * R2, D)
    a2r = np.concatenate([a2, np.asarray(L0_cond2_Wr)], 0).T
    b2 = np.asarray(L0_cond2_B).transpose(1, 0, 2).reshape(D, E2 * R2)
    bf = np.asarray(L0_ffn_Bf).transpose(0, 2, 1).reshape(EF * 16, D)
    lang = np.asarray(itok_B_0_7).reshape(PAIRS, 2, SEQ_PER_TILE, 1)
    lang = np.broadcast_to(lang, (PAIRS, 2, SEQ_PER_TILE, S)).reshape(PAIRS, 2, P).transpose(0, 2, 1)

    inv = (1.0 / 10000.0 ** (np.arange(0, HD, 2, dtype=np.float32) / np.float32(HD))).astype(np.float32)
    ang = np.outer(np.arange(S, dtype=np.float32), inv)
    c, s_ = np.cos(ang), np.sin(ang)
    consts = np.zeros((P, K_ALL), np.float32)
    consts[:, K_COS:K_COS + HD] = np.tile(np.concatenate([c, c], 1), (SEQ_PER_TILE, 1))
    consts[:, K_SIN:K_SIN + HD] = np.tile(np.concatenate([-s_, s_], 1), (SEQ_PER_TILE, 1))
    consts[:, K_MASK:K_MASK + S] = np.tile(np.triu(np.full((S, S), MASKED, np.float32), 1), (REP, 1))
    consts[:, K_IOTA:K_IOTA + E2] = np.arange(E2)
    consts[:, K_ID:K_ID + P] = np.eye(P)

    given = {
        "x": x,
        "xT": np.ascontiguousarray(x.reshape(NSEQ * S, D).T),
        "cond": np.ascontiguousarray(itok_B_0_15),
        "lang": np.ascontiguousarray(lang),
        "wcond": np.ascontiguousarray(L0_cond_weights),
        "wqkv": chunked(qkv_rows.T),
        "wo": chunked(o_cols),
        "w2": chunked(L0_cond2_W),
        "a2r": chunked(a2r),
        "b2": chunked(b2),
        "wf": chunked(np.asarray(L0_ffn_W).T),
        "af": chunked(np.asarray(L0_ffn_A).reshape(EF * 16, D), 2),
        "bf": chunked(bf, 2),
        "coeffs": np.ascontiguousarray(np.repeat(np.asarray(L0_ffn_coeffs), 16).reshape(2, P).T),
        "scales": np.ascontiguousarray(np.repeat(np.asarray(L0_ffn_scales), 16).reshape(2, P).T),
        "bias": np.ascontiguousarray(L0_ffn_bias),
        "consts": consts,
    }
    nc = _bacc.Bacc("TRN2", target_bir_lowering=False, num_devices=1)
    arrays, args = {}, {}
    for name, a in given.items():
        arrays[f"{name}_dram"] = a
        args[name] = nc.dram_tensor(f"{name}_dram", a.shape, mybir.dt.from_np(a.dtype), kind="ExternalInput").ap()
    out = nc.dram_tensor("out_dram", _OUT, F32, kind="ExternalOutput").ap()
    program(nc, out=out, **args)
    r = _run(nc, [arrays], core_ids=[0])
    return r.results[0]["out_dram"]
```

```python
from contextlib import ExitStack

import concourse.bass as bass
from concourse import mybir
import numpy as np

P = 128
NSEQ, S, D = 64, 32, 512
SEQ_PER_TILE = P // S
TILES = NSEQ // SEQ_PER_TILE
PAIRS = TILES // 2
SLOTS = 2 * SEQ_PER_TILE
HKV, REP, HD = 8, 4, 16
C = D // P
QKV = D + 2 * HKV * HD
E2, R2 = 8, 16
EF = 16
ROUT = E2 * R2 + E2
FW = ROUT + D
HALF = FW // 2
OUT_A = HALF - ROUT
LANG_BIAS = 5.0
SCALING = 2.0
MASKED = -1.0e30
GATE_STEPS = 11

F32 = mybir.dt.float32
F32R = mybir.dt.float32r
I32 = mybir.dt.int32
U32 = mybir.dt.uint32
ALU = mybir.AluOpType
ACT = mybir.ActivationFunctionType
AX = mybir.AxisListType

K_COS, K_SIN, K_MASK, K_IOTA, K_ID = 0, HD, 2 * HD, 2 * HD + S, 2 * HD + S + E2
K_ALL = K_ID + P

LOOP_FROM, LOOP_TO = 2, PAIRS - 2


def program(nc, x, xT, cond, lang, wcond, wqkv, wo, w2, a2r, b2, wf, af, bf, coeffs, scales, bias, consts, out):
    x_t = x.rearrange("(n b) c f -> n (b c) f", b=SEQ_PER_TILE)
    out_t = out.rearrange("(n b) c f -> n (b c) f", b=SEQ_PER_TILE)
    xT_p = xT.rearrange("(c p) n -> p c n", p=P)

    ctx = ExitStack()
    with ctx:
        def sb(name, shape, dt=F32):
            return ctx.enter_context(nc.sbuf_tensor(name, shape, dt))

        def pb(name, shape):
            return ctx.enter_context(nc.psum_tensor(name, shape, F32))

        def sem(name):
            return ctx.enter_context(nc.semaphore(name))

        def pair_of(name, shape):
            return sb(name + "_hi", shape, F32R), sb(name + "_lo", shape, F32R)

        const = sb("const", [P, K_ALL])
        cos = const[:, K_COS:K_COS + HD]
        sin = const[:, K_SIN:K_SIN + HD]
        mask = const[:, K_MASK:K_MASK + S]
        iota = const[:, K_IOTA:K_IOTA + E2]
        ident = const[:, K_ID:K_ID + P]
        cond_sb = sb("cond_sb", [1, NSEQ], I32)
        wqkv_raw = sb("wqkv_raw", [P, C, QKV])
        wqkv_hi, wqkv_lo = pair_of("wqkv", [P, C, QKV])
        wo_raw = sb("wo_raw", [P, C, D])
        wo_hi, wo_lo = pair_of("wo", [P, C, D])
        w2_sb = sb("w2_sb", [P, C, D])
        wf_sb = sb("wf_sb", [P, C, D])
        wfull = sb("wfull", [P, C, D])
        a2r_sb = sb("a2r_sb", [P, C, ROUT])
        b2_sb = sb("b2_sb", [P, C, E2 * R2])
        af_sb = sb("af_sb", [P, 2, D])
        bf_sb = sb("bf_sb", [P, 2, D])
        cw = sb("cw", [P, 3, 2])
        bias_sb = sb("bias_sb", [P, D])
        fused = sb("fused", [P, 2, D])
        fw_hi, fw_lo = pair_of("fw", [P, C, FW])
        bc_hi, bc_lo = pair_of("bc", [P, D])
        xt = sb("xt", [P, 2, D])
        wbd = sb("wbd", [P, 2, P])
        hT_hi, hT_lo = pair_of("hT", [P, 2, C, P])
        rope_cos = sb("rope_cos", [P, 5, P])
        rope_sin = sb("rope_sin", [P, 5, P])
        qk = sb("qk", [P, 5, P])
        vst = sb("vst", [P, 2, P])
        kst = sb("kst", [P, 2, P])
        QT = sb("QT", [P, 2, SEQ_PER_TILE, REP, S])
        Kbd = sb("Kbd", [P, 2, HKV, P])
        Vbd = sb("Vbd", [P, 2, SEQ_PER_TILE, 2, 64])
        v_dram = nc.dram_tensor("v_scratch", [2, P, P], F32).ap()
        att = sb("att", [P, 4, HKV, S])
        rowmax = sb("rowmax", [P, 2, HKV])
        rowsum = sb("rowsum", [P, 2, HKV])
        rowinv = sb("rowinv", [P, 2, HKV])
        PTs = sb("PTs", [P, 2, 2, P])
        oT_hi, oT_lo = pair_of("oT", [P, REP, 2, SEQ_PER_TILE, S])
        xres = sb("xres", [P, C, 2 * P])
        x1 = sb("x1", [P, C, 2 * P])
        x1_hi, x1_lo = pair_of("x1T", [P, C, 2 * P])
        ids = sb("ids", [P, 2], I32)
        lbias = sb("lbias", [P, E2])
        logits = sb("logits", [P, E2])
        top8 = sb("top8", [P, E2])
        idx8 = sb("idx8", [P, E2], U32)
        idxf = sb("idxf", [P, 2])
        gs = sb("gs", [P, 8])
        first = sb("first", [P, E2])
        second = sb("second", [P, E2])
        gates = sb("gates", [P, E2])
        gh = sb("gh", [P, E2 * R2])
        ghT_hi, ghT_lo = pair_of("ghT", [P, P])
        y = sb("y", [P, 2, D])

        b_mix = pb("b_mix", [P, 512])
        b_qkv = pb("b_qkv", [P, 1024])
        b_out0 = pb("b_out0", [P, 512])
        b_out1 = pb("b_out1", [P, 512])
        b_s = pb("b_s", [P, 512])
        b_pt = pb("b_pt", [P, 512])
        b_o = pb("b_o", [P, 512])
        b_out = [b_out0, b_out1]

        names = """const_in cond_in wqkv_in wo_in prep_in bias_in zeroed wqkv_h wqkv_l wo_h wo_l
            scaled wprod wfull_sb fused_sb fused_h fused_l a2r_h a2r_l
            mixed hT_h hT_l q_done kv_done rope_terms roped v_out qT kT qT_sb kT_sb
            scored masked maxed shifted expd summed inverted normed pT pT_sb pv oT_h oT_l
            wo_done x1_sum x1_h x1_l fin gate_steps gate_exp gated ghT ghT_h ghT_l fin2 y_sb
            xres_in ids_in sp_passed"""
        sm = {n: sem(n) for n in names.split()}
        x_in = [sem(f"x_in{t}") for t in range(2)]
        w_in = [sem(f"w_in{t}") for t in range(2)]
        v_scr = [sem(f"v_scr{t}") for t in range(2)]
        v_in = [sem(f"v_in{t}") for t in range(2)]
        k_in = [sem(f"k_in{t}") for t in range(2)]
        stored = [sem(f"stored{t}") for t in range(2)]

        def steps(engine, body):
            for i in range(-2, LOOP_FROM):
                body(i, i)
            with engine.Fori(LOOP_FROM, LOOP_TO) as i:
                body(i, LOOP_FROM)
            for i in range(LOOP_TO, PAIRS + 2):
                body(i, i)

        def pair(k):
            return 0 <= k < PAIRS

        block = ctx.enter_context(nc.Block())

        @block.sync
        def _(sp):
            sp.dma_start(cond_sb[0:1, :], cond.rearrange("(a n) -> a n", a=1)).then_inc(sm["cond_in"], 16)
            sp.dma_start(const[:, :], consts).then_inc(sm["const_in"], 16)
            sp.wait_ge(sm["cond_in"], 16)
            sp.wait_ge(sm["zeroed"], 3)

            def settled():
                sp.wait_ge(sm["cond_in"], 16)

            def load_x(n, t):
                settled()
                sp.dma_start(xt[:, t, :], x_t[2 * n + t]).then_inc(x_in[t], 16)
                for b in range(SEQ_PER_TILE):
                    at = 8 * n + 4 * t + b
                    which = sp.value_load(cond_sb[0:1, bass.ds(at, 1)], min_val=0, max_val=15)
                    sp.dma_start(wbd[S * b:S * b + S, t, S * b:S * b + S],
                                 wcond[bass.ds(which, 1)].rearrange("a c d -> (a c) d")).then_inc(w_in[t], 16)

            def spread_v(t):
                src = v_dram[t].rearrange("(k b) (h g d) -> k (b h) g d", b=SEQ_PER_TILE, h=2, g=4)
                for g in range(4):
                    dst = Vbd[S * g:S * g + S, t, :, :, HD * g:HD * g + HD]
                    sp.dma_start(dst.rearrange("p b h d -> p (b h) d"), src[:, :, g, :]).then_inc(v_in[t], 16)

            def passed():
                sp.sem_inc(sm["sp_passed"], 1)

            def v_to_dram(n, k, t):
                sp.wait_ge(sm["v_out"], 2 * n + t + 1)
                if k > 0:
                    passed()
                    sp.wait_ge(v_in[t], 64 * n)
                sp.dma_start(v_dram[t].rearrange("(k b) c -> b k c", b=SEQ_PER_TILE),
                             vst[:, t, :]).then_inc(v_scr[t], 16)

            def spread_k(n, k, t):
                sp.wait_ge(sm["kT_sb"], 2 * n + t + 1)
                for g in range(HKV):
                    r = slice(HD * g, HD * g + HD)
                    sp.dma_start(Kbd[r, t, g, :], kst[r, t, :]).then_inc(k_in[t], 16)

            def body(i, k):
                if pair(k + 2):
                    if k > -2:
                        sp.wait_ge(sm["mixed"], 2 * (i + 1) + 1)
                    load_x(i + 2, 0)
                if pair(k - 1):
                    if k > 1:
                        sp.wait_ge(sm["gated"], 2 * (i - 2) + 2)
                    settled()
                    sp.dma_start(ids[:, :], lang[i - 1]).then_inc(sm["ids_in"], 16)
                if pair(k):
                    sp.wait_ge(v_scr[1], 16 * (i + 1))
                    if k > 0:
                        passed()
                        sp.wait_ge(sm["pv"], 8 * i)
                    spread_v(1)
                if pair(k - 2):
                    sp.wait_ge(sm["y_sb"], 2 * (2 * (i - 2) + 2))
                    settled()
                    sp.dma_start(out_t[2 * (i - 2) + 1], y[:, 1, :]).then_inc(stored[1], 16)
                if pair(k + 1):
                    v_to_dram(i + 1, k + 1, 0)
                if pair(k + 2):
                    if k > -2:
                        sp.wait_ge(sm["mixed"], 2 * (i + 1) + 2)
                    load_x(i + 2, 1)
                if pair(k + 1):
                    spread_k(i + 1, k + 1, 0)
                if pair(k):
                    if k > 0:
                        sp.wait_ge(sm["x1_sum"], 2 * (i - 1) + 2)
                    settled()
                    sp.dma_start(xres[:, :, :], xT_p[:, :, bass.ds(i * (2 * P), 2 * P)]).then_inc(sm["xres_in"], 16)
                if pair(k + 1):
                    sp.wait_ge(v_scr[0], 16 * (i + 2))
                    if k >= 0:
                        passed()
                        sp.wait_ge(sm["pv"], 8 * i + 4)
                    spread_v(0)
                    v_to_dram(i + 1, k + 1, 1)
                if pair(k - 1):
                    sp.wait_ge(sm["y_sb"], 2 * (2 * (i - 1) + 1))
                    settled()
                    sp.dma_start(out_t[2 * (i - 1)], y[:, 0, :]).then_inc(stored[0], 16)
                if pair(k + 1):
                    spread_k(i + 1, k + 1, 1)

            steps(sp, body)
            for t in range(2):
                sp.wait_ge(stored[t], 16 * PAIRS)
                sp.wait_ge(v_scr[t], 16 * PAIRS)

        @block.gpsimd
        def _(pool):
            nc.gpsimd.memset(wbd[:, :, :], 0.0).then_inc(sm["zeroed"], 1)
            nc.gpsimd.memset(Kbd[:, :, :, :], 0.0).then_inc(sm["zeroed"], 1)
            nc.gpsimd.memset(Vbd[:, :, :, :, :], 0.0).then_inc(sm["zeroed"], 1)

            def subtract(dst, full, high, signal):
                nc.gpsimd.tensor_tensor(dst, full, high.bitcast(F32), ALU.subtract).then_inc(signal, 1)

            def shift(i, s):
                pool.wait_ge(sm["maxed"], 8 * i + s + 1)
                m = rowmax[:, s % 2, :].unsqueeze(2).broadcast_to([P, HKV, S])
                nc.gpsimd.tensor_tensor(att[:, s % 4], att[:, s % 4], m, ALU.subtract).then_inc(sm["shifted"], 1)

            def normalise(i, s):
                pool.wait_ge(sm["inverted"], 8 * i + s + 1)
                r = rowinv[:, s % 2, :].unsqueeze(2).broadcast_to([P, HKV, S])
                nc.gpsimd.tensor_tensor(att[:, s % 4], att[:, s % 4], r, ALU.mult).then_inc(sm["normed"], 1)

            def rope_sum(n, t):
                pool.wait_ge(sm["rope_terms"], 3 * (2 * n + t) + 3)
                nc.gpsimd.tensor_tensor(qk[:, :, :], rope_cos[:, :, :], rope_sin[:, :, :],
                                        ALU.add).then_inc(sm["roped"], 1)

            def x1_low(p, h):
                pool.wait_ge(sm["x1_h"], 2 * p + h + 1)
                subtract(x1_lo[:, 2 * h:2 * h + 2, :], x1[:, 2 * h:2 * h + 2, :],
                         x1_hi[:, 2 * h:2 * h + 2, :], sm["x1_l"])

            def fused_low(m):
                pool.wait_ge(sm["fused_h"], m + 1)
                if m < C:
                    subtract(fw_lo[:, m, ROUT:FW], fused[:, m % 2, :], fw_hi[:, m, ROUT:FW], sm["fused_l"])
                else:
                    subtract(bc_lo[:, :], fused[:, m % 2, :], bc_hi[:, :], sm["fused_l"])

            def body(i, k):
                for s in range(SLOTS):
                    if pair(k):
                        shift(i, s)
                    if s == 2 and pair(k + 1):
                        rope_sum(i + 1, 0)
                    if s == 7 and pair(k + 1):
                        rope_sum(i + 1, 1)
                    if s == 3 and pair(k - 1):
                        x1_low(i - 1, 0)
                    if pair(k):
                        normalise(i, s)
                    if s == 3 and pair(k - 1):
                        x1_low(i - 1, 1)
                    if k == 0 and s == 0:
                        pool.wait_ge(sm["wo_h"], 1)
                        subtract(wo_lo[:, :, :], wo_raw[:, :, :], wo_hi[:, :, :], sm["wo_l"])
                        pool.wait_ge(sm["a2r_h"], 1)
                        subtract(fw_lo[:, :, 0:ROUT], a2r_sb[:, :, :], fw_hi[:, :, 0:ROUT], sm["a2r_l"])
                    if k == 0 and 4 <= s:
                        fused_low(s - 4)
                if k == 0:
                    fused_low(C)

            steps(pool, body)

        @block.scalar
        def _(act):
            act.dma_start(wqkv_raw[:, 0:2, :], wqkv[:, 0:2, :]).then_inc(sm["wqkv_in"], 16)
            act.dma_start(wqkv_raw[:, 2:4, :], wqkv[:, 2:4, :]).then_inc(sm["wqkv_in"], 16)
            act.dma_start(wo_raw[:, :, :], wo).then_inc(sm["wo_in"], 16)
            for dst, src in ((af_sb[:, :, :], af), (bf_sb[:, :, :], bf), (wf_sb[:, :, :], wf),
                             (w2_sb[:, :, :], w2), (b2_sb[:, :, :], b2), (a2r_sb[:, :, :], a2r),
                             (cw[:, 0, :], coeffs), (cw[:, 1, :], scales)):
                act.dma_start(dst, src).then_inc(sm["prep_in"], 16)
            act.dma_start(bias_sb[:, :], bias.rearrange("(a n) -> a n", a=1).broadcast_to([P, D])
                          ).then_inc(sm["bias_in"], 16)
            act.wait_ge(sm["wqkv_in"], 32)
            for c in range(C):
                nc.scalar.copy(wqkv_hi[:, c, :], wqkv_raw[:, c, :]).then_inc(sm["wqkv_h"], 1)

            def mix_high(n, t):
                act.wait_ge(sm["mixed"], 2 * n + t + 1)
                nc.scalar.copy(hT_hi[:, t].rearrange("p c n -> p (c n)"), b_mix[:, :]).then_inc(sm["hT_h"], 1)

            def value_copy(n, k, t):
                act.wait_ge(sm["kv_done"], 2 * n + t + 1)
                if k > 0:
                    act.wait_ge(v_scr[t], 16 * n)
                nc.scalar.copy(vst[:, t, :], b_qkv[:, D + P:D + 2 * P]).then_inc(sm["v_out"], 1)

            def qk_copy(n, k, t):
                act.wait_ge(sm["qT"], 2 * n + t + 1)
                src = b_qkv[:, 0:D].rearrange("p (r b s) -> p b r s", r=REP, b=SEQ_PER_TILE)
                nc.scalar.copy(QT[:, t], src).then_inc(sm["qT_sb"], 1)
                act.wait_ge(sm["kT"], 2 * n + t + 1)
                if k > 0:
                    act.wait_ge(k_in[t], 128 * n)
                nc.scalar.copy(kst[:, t, :], b_qkv[:, D:D + P]).then_inc(sm["kT_sb"], 1)

            def probs_T_copy(i, k, s):
                act.wait_ge(sm["pT"], 8 * i + s + 1)
                if k > 0 or s >= 2:
                    act.wait_ge(sm["pv"], 8 * i + s - 1)
                nc.scalar.copy(PTs[:, s % 2].rearrange("p h n -> p (h n)"), b_pt[:, 0:2 * P]).then_inc(sm["pT_sb"], 1)

            def exps(i, s):
                act.wait_ge(sm["shifted"], 8 * i + s + 1)
                nc.scalar.activation(att[:, s % 4], att[:, s % 4], ACT.Exp,
                                     scale=float(HD) ** -0.5).then_inc(sm["expd"], 1)

            def o_high(i, t):
                act.wait_ge(sm["pv"], 8 * i + 4 * t + 4)
                src = b_o[:, :].rearrange("p (b r s) -> p r b s", b=SEQ_PER_TILE, r=REP)
                nc.scalar.copy(oT_hi[:, :, t], src).then_inc(sm["oT_h"], 1)

            def x1_high(p, h):
                act.wait_ge(sm["x1_sum"], 2 * p + h + 1)
                nc.scalar.copy(x1_hi[:, 2 * h:2 * h + 2, :], x1[:, 2 * h:2 * h + 2, :]).then_inc(sm["x1_h"], 1)

            def gate_exp(p, t):
                act.wait_ge(sm["gate_steps"], GATE_STEPS * (2 * p + t) + 4)
                nc.scalar.activation(gs[:, 1:2], gs[:, 0:1], ACT.Exp).then_inc(sm["gate_exp"], 1)

            def gh_high(p, t):
                act.wait_ge(sm["ghT"], 2 * p + t + 1)
                nc.scalar.copy(ghT_hi[:, :], b_mix[:, 0:P]).then_inc(sm["ghT_h"], 1)

            def fused_high(m):
                act.wait_ge(sm["fused_sb"], 2 * m + 2 if m < C else 2 * C + 1)
                dst = fw_hi[:, m, ROUT:FW] if m < C else bc_hi[:, :]
                nc.scalar.copy(dst, fused[:, m % 2, :]).then_inc(sm["fused_h"], 1)

            def body(i, k):
                for s in range(SLOTS):
                    if s == 6 and pair(k):
                        o_high(i, 0)
                    if s < 2:
                        if pair(k - 1):
                            probs_T_copy(i - 1, k - 1, SLOTS - 2 + s)
                    elif pair(k):
                        probs_T_copy(i, k, s - 2)
                    if s == 1 and pair(k - 2):
                        gh_high(i - 2, 1)
                    if s == 2 and pair(k + 1):
                        mix_high(i + 1, 1)
                    if s == 3 and pair(k + 1):
                        qk_copy(i + 1, k + 1, 0)
                    if s == 3 and pair(k - 1):
                        x1_high(i - 1, 0)
                    if pair(k):
                        exps(i, s)
                    if s == 0 and pair(k - 2):
                        gate_exp(i - 2, 1)
                    if s == 1 and pair(k - 1):
                        o_high(i - 1, 1)
                    if s == 1 and pair(k + 1):
                        value_copy(i + 1, k + 1, 0)
                    if s == 3 and pair(k - 1):
                        x1_high(i - 1, 1)
                    if s == 5 and pair(k - 1):
                        gate_exp(i - 1, 0)
                    if s == 6:
                        if pair(k + 1):
                            value_copy(i + 1, k + 1, 1)
                        if pair(k - 1):
                            gh_high(i - 1, 0)
                    if s == 7 and pair(k + 2):
                        mix_high(i + 2, 0)
                    if s == 7 and pair(k + 1):
                        qk_copy(i + 1, k + 1, 1)
                    if s == 0 and k == 0:
                        act.wait_ge(sm["wo_in"], 16)
                        nc.scalar.copy(wo_hi[:, :, :], wo_raw[:, :, :]).then_inc(sm["wo_h"], 1)
                        act.wait_ge(sm["prep_in"], 16 * 8)
                        nc.scalar.copy(fw_hi[:, :, 0:ROUT], a2r_sb[:, :, :]).then_inc(sm["a2r_h"], 1)
                    if k == 0 and 4 <= s:
                        fused_high(s - 4)
                if k == 0:
                    fused_high(C)

            steps(act, body)

        @block.vector
        def _(dve):
            def low(dst, full, high, signal):
                nc.vector.tensor_tensor(dst, full, high.bitcast(F32), ALU.subtract).then_inc(signal, 1)

            def mix_low(n, t):
                dve.wait_ge(sm["hT_h"], 2 * n + t + 1)
                low(hT_lo[:, t].rearrange("p c n -> p (c n)"), b_mix[:, :],
                    hT_hi[:, t].rearrange("p c n -> p (c n)"), sm["hT_l"])

            def rope_products(n, k, t):
                dve.wait_ge(sm["q_done"], 2 * n + t + 1)
                dve.wait_ge(sm["v_out"], 2 * n + t + 1)
                if k > 0 or t > 0:
                    dve.wait_ge(sm["roped"], 2 * n + t)
                heads = (D + P) // HD
                q = b_qkv[:, 0:D + P].rearrange("p (h d) -> p h d", d=HD)
                c_out = rope_cos[:, :, :].rearrange("p c (h d) -> p (c h) d", d=HD)
                s_out = rope_sin[:, :, :].rearrange("p c (h d) -> p (c h) d", d=HD)
                half = HD // 2
                nc.vector.tensor_tensor(c_out, q, cos.unsqueeze(1).broadcast_to([P, heads, HD]),
                                        ALU.mult).then_inc(sm["rope_terms"], 1)
                for lo, hi in ((0, half), (half, 0)):
                    nc.vector.tensor_tensor(s_out[:, :, lo:lo + half], q[:, :, hi:hi + half],
                                            sin[:, lo:lo + half].unsqueeze(1).broadcast_to([P, heads, half]),
                                            ALU.mult).then_inc(sm["rope_terms"], 1)

            def mask_and_max(i, k, s):
                dve.wait_ge(sm["scored"], 8 * i + s + 1)
                m = mask.unsqueeze(1).broadcast_to([P, HKV, S])
                nc.vector.tensor_tensor(att[:, s % 4], b_s[:, 0:HKV * S].rearrange("p (g k) -> p g k", g=HKV), m,
                                        ALU.add).then_inc(sm["masked"], 1)
                dve.wait_ge(sm["masked"], 8 * i + s + 1)
                nc.vector.tensor_reduce(rowmax[:, s % 2, :], att[:, s % 4], AX.X, ALU.max).then_inc(sm["maxed"], 1)

            def row_sums(i, s):
                dve.wait_ge(sm["expd"], 8 * i + s + 1)
                nc.vector.tensor_reduce(rowsum[:, s % 2, :], att[:, s % 4], AX.X, ALU.add).then_inc(sm["summed"], 1)
                dve.wait_ge(sm["summed"], 8 * i + s + 1)
                nc.vector.reciprocal(rowinv[:, s % 2, :], rowsum[:, s % 2, :]).then_inc(sm["inverted"], 1)

            def o_low(i, t):
                dve.wait_ge(sm["oT_h"], 2 * i + t + 1)
                src = b_o[:, :].rearrange("p (b r s) -> p r b s", b=SEQ_PER_TILE, r=REP)
                low(oT_lo[:, :, t], src, oT_hi[:, :, t], sm["oT_l"])

            def add_residual(p, h):
                dve.wait_ge(sm["wo_done"], 2 * p + h + 1)
                dve.wait_ge(sm["xres_in"], 16 * (p + 1))
                nc.vector.tensor_tensor(x1[:, 2 * h:2 * h + 2, :], b_out[h][:, :].rearrange("p (c n) -> p c n", c=2),
                                        xres[:, 2 * h:2 * h + 2, :], ALU.add).then_inc(sm["x1_sum"], 1)

            def gating(p, t):
                done = [GATE_STEPS * (2 * p + t)]

                def count(instruction):
                    done[0] = done[0] + 1
                    instruction.then_inc(sm["gate_steps"], 1)

                def step(instruction):
                    count(instruction)
                    dve.wait_ge(sm["gate_steps"], done[0])

                dve.wait_ge(sm["ids_in"], 16 * (p + 1))
                step(nc.vector.tensor_scalar(lbias[:, :], iota, ids[:, t:t + 1], LANG_BIAS, ALU.is_equal, ALU.mult))
                dve.wait_ge(sm["fin"], 2 * p + t + 1)
                step(nc.vector.tensor_tensor(logits[:, :], b_out0[:, E2 * R2:ROUT], lbias[:, :], ALU.add))
                nc.vector.tensor_copy(gs[:, 6:7], logits[:, 0:1])
                step(nc.vector.max(top8[:, :], logits[:, :]))
                count(nc.vector.tensor_tensor(gs[:, 0:1], top8[:, 1:2], top8[:, 0:1], ALU.subtract))
                step(nc.vector.max_index(idx8[:, :], top8[:, :], logits[:, :]))
                step(nc.vector.tensor_copy(idxf[:, :], idx8[:, 0:2]))
                count(nc.vector.tensor_scalar(first[:, :], iota, idxf[:, 0:1], None, ALU.is_equal))
                dve.wait_ge(sm["gate_exp"], 2 * p + t + 1)
                count(nc.vector.tensor_scalar(gs[:, 2:3], gs[:, 1:2], 1.0 / SCALING, 1.0 / SCALING, ALU.mult, ALU.add))
                step(nc.vector.tensor_scalar(second[:, :], iota, idxf[:, 1:2], gs[:, 1:2], ALU.is_equal, ALU.mult))
                count(nc.vector.reciprocal(gs[:, 3:4], gs[:, 2:3]))
                step(nc.vector.tensor_tensor(gates[:, :], first[:, :], second[:, :], ALU.add))
                nc.vector.scalar_tensor_tensor(out=gh[:, :].rearrange("p (e r) -> p e r", e=E2),
                                               in0=b_out0[:, 0:E2 * R2].rearrange("p (e r) -> p e r", e=E2),
                                               scalar=gs[:, 3:4], in1=gates[:, :].unsqueeze(2).broadcast_to([P, E2, R2]),
                                               op0=ALU.mult, op1=ALU.mult).then_inc(sm["gated"], 1)

            def gh_low(p, t):
                dve.wait_ge(sm["ghT_h"], 2 * p + t + 1)
                low(ghT_lo[:, :], b_mix[:, 0:P], ghT_hi[:, :], sm["ghT_l"])

            def finish(p, k, t):
                dve.wait_ge(sm["fin2"], 2 * p + t + 1)
                if k > 0:
                    dve.wait_ge(stored[t], 16 * p)
                nc.vector.tensor_tensor(y[:, t, 0:OUT_A], b_out0[:, ROUT:HALF], bias_sb[:, 0:OUT_A],
                                        ALU.add).then_inc(sm["y_sb"], 1)
                nc.vector.tensor_tensor(y[:, t, OUT_A:D], b_out1[:, 0:HALF], bias_sb[:, OUT_A:D],
                                        ALU.add).then_inc(sm["y_sb"], 1)

            def full_weight(m):
                dve.wait_ge(sm["wprod"], m + 1)
                nc.vector.tensor_tensor(wfull[:, m, :], b_out[m % 2][:, :], wf_sb[:, m, :],
                                        ALU.add).then_inc(sm["wfull_sb"], 1)

            def fused_weight(m):
                dve.wait_ge(sm["wprod"], C + m + 1)
                if m >= 2:
                    dve.wait_ge(sm["fused_l"], m - 1)
                nc.vector.tensor_copy(fused[:, m % 2, :], b_out[m % 2][:, :]).then_inc(sm["fused_sb"], 1)
                if m < C:
                    dve.wait_ge(sm["fused_sb"], 2 * m + 1)
                    block_m = fused[:, m % 2, P * m:P * m + P]
                    nc.vector.tensor_tensor(block_m, block_m, ident, ALU.add).then_inc(sm["fused_sb"], 1)

            def body(i, k):
                for s in range(SLOTS):
                    if pair(k):
                        mask_and_max(i, k, s)
                    if s == 7 and pair(k - 1):
                        finish(i - 1, k - 1, 0)
                    if s == 0 and pair(k - 2):
                        gating(i - 2, 1)
                    if s == 1 and pair(k - 2):
                        gh_low(i - 2, 1)
                    if s == 1 and pair(k - 1):
                        o_low(i - 1, 1)
                    if s == 2 and pair(k + 1):
                        rope_products(i + 1, k + 1, 0)
                    if s == 3 and pair(k + 1):
                        mix_low(i + 1, 1)
                    if s == 3 and pair(k - 1):
                        add_residual(i - 1, 0)
                    if s == 6 and pair(k):
                        o_low(i, 0)
                    if s == 7 and pair(k + 1):
                        rope_products(i + 1, k + 1, 1)
                    if pair(k):
                        row_sums(i, s)
                    if s == 1 and pair(k - 2):
                        finish(i - 2, k - 2, 1)
                    if s == 3 and pair(k - 1):
                        add_residual(i - 1, 1)
                    if s == 5 and pair(k - 1):
                        gating(i - 1, 0)
                    if s == 6 and pair(k - 1):
                        gh_low(i - 1, 0)
                    if s == 7 and pair(k + 2):
                        mix_low(i + 2, 0)
                    if k == 0 and s == 0:
                        dve.wait_ge(sm["prep_in"], 16 * 8)
                        nc.vector.tensor_tensor(cw[:, 2, :], cw[:, 0, :], cw[:, 1, :], ALU.mult).then_inc(sm["scaled"], 1)
                        dve.wait_ge(sm["scaled"], 1)
                        for e in range(2):
                            nc.vector.tensor_scalar(bf_sb[:, e, :], bf_sb[:, e, :], cw[:, 2, e:e + 1], None,
                                                    ALU.mult).then_inc(sm["scaled"], 1)
                    if k == 0 and s in (1, 2):
                        full_weight(2 * s - 2)
                        full_weight(2 * s - 1)
                    if k == 0 and s == 3:
                        fused_weight(0)
                    if k == 0 and s >= 4:
                        fused_weight(s - 3)

            dve.wait_ge(sm["const_in"], 16)
            dve.wait_ge(sm["bias_in"], 16)
            for c in range(C):
                dve.wait_ge(sm["wqkv_h"], c + 1)
                low(wqkv_lo[:, c, :], wqkv_raw[:, c, :], wqkv_hi[:, c, :], sm["wqkv_l"])
            steps(dve, body)

        @block.tensor
        def _(pe):
            def split_product(dst, chunks, first=True, final=True):
                for c, (sh, sl, mh, ml) in enumerate(chunks):
                    for n, (a, b) in enumerate(((sh, mh), (sh, ml), (sl, mh))):
                        last = nc.tensor.matmul(dst, a, b, start=(first and c == 0 and n == 0),
                                                stop=(final and c == len(chunks) - 1 and n == 2))
                return last

            def mix(n, t):
                pe.wait_ge(x_in[t], 16 * (n + 1))
                pe.wait_ge(w_in[t], 64 * (n + 1))
                for c in range(C):
                    last = nc.tensor.matmul(b_mix[:, P * c:P * c + P], xt[:, t, P * c:P * c + P], wbd[:, t, :],
                                            start=True, stop=True)
                last.then_inc(sm["mixed"], 1)

            def project_q(n, k, t, part):
                if part == 0:
                    pe.wait_ge(sm["hT_l"], 2 * n + t + 1)
                    if k > 0 or t > 0:
                        pe.wait_ge(sm["qT_sb"], 2 * n + t)
                chunks = [(hT_hi[:, t, c], hT_lo[:, t, c], wqkv_hi[:, c, 0:D], wqkv_lo[:, c, 0:D])
                          for c in (2 * part, 2 * part + 1)]
                last = split_product(b_qkv[:, 0:D], chunks, part == 0, part == 1)
                if part == 1:
                    last.then_inc(sm["q_done"], 1)

            def project_kv(n, k, t):
                if k > 0 or t > 0:
                    pe.wait_ge(sm["kT_sb"], 2 * n + t)
                split_product(b_qkv[:, D:QKV], [(hT_hi[:, t, c], hT_lo[:, t, c], wqkv_hi[:, c, D:QKV],
                                                 wqkv_lo[:, c, D:QKV]) for c in range(C)]).then_inc(sm["kv_done"], 1)

            def transpose_qk(n, t):
                pe.wait_ge(sm["roped"], 2 * n + t + 1)
                for r in range(REP):
                    last = nc.tensor.transpose(b_qkv[:, P * r:P * r + P], qk[:, r, :], ident)
                last.then_inc(sm["qT"], 1)
                pe.wait_ge(sm["v_out"], 2 * n + t + 1)
                nc.tensor.transpose(b_qkv[:, D:D + P], qk[:, REP, :], ident).then_inc(sm["kT"], 1)

            def scores(i, k, s):
                t, b = s // SEQ_PER_TILE, s % SEQ_PER_TILE
                if b == 0:
                    pe.wait_ge(k_in[t], 128 * (i + 1))
                    pe.wait_ge(sm["qT_sb"], 2 * i + t + 1)
                if k > 0 or s > 0:
                    pe.wait_ge(sm["masked"], 8 * i + s)
                nc.tensor.matmul(b_s[:, 0:HKV * S], QT[:, t, b].rearrange("p r s -> p (r s)"),
                                 Kbd[:, t, :, S * b:S * b + S], start=True, stop=True).then_inc(sm["scored"], 1)

            def probs_T(i, k, s):
                pe.wait_ge(sm["normed"], 8 * i + s + 1)
                if k > 0 or s > 0:
                    pe.wait_ge(sm["pT_sb"], 8 * i + s)
                for h in range(2):
                    last = nc.tensor.transpose(b_pt[:, P * h:P * h + P],
                                               att[:, s % 4, 4 * h:4 * h + 4].rearrange("p g k -> p (g k)"), ident)
                last.then_inc(sm["pT"], 1)

            def values(i, k, s):
                t, b = s // SEQ_PER_TILE, s % SEQ_PER_TILE
                pe.wait_ge(sm["pT_sb"], 8 * i + s + 1)
                if b == 0:
                    pe.wait_ge(v_in[t], 64 * (i + 1))
                    if k > 0 or t > 0:
                        pe.wait_ge(sm["oT_l"], 2 * i + t)
                for h in range(2):
                    last = nc.tensor.matmul(b_o[64 * h:64 * h + 64, P * b:P * b + P], Vbd[:, t, b, h, :],
                                            PTs[:, s % 2, h, :], start=True, stop=True)
                last.then_inc(sm["pv"], 1)

            def output_projection(p, k, c):
                if c == 0:
                    if k > 0:
                        pe.wait_ge(sm["y_sb"], 4 * p)
                    else:
                        pe.wait_ge(sm["fused_sb"], 2 * C + 1)
                        pe.wait_ge(sm["wo_l"], 1)
                    pe.wait_ge(sm["oT_l"], 2 * p + 2)
                o = [(wo_hi[:, r, P * c:P * c + P], wo_lo[:, r, P * c:P * c + P],
                      oT_hi[:, r].rearrange("p t b s -> p (t b s)"), oT_lo[:, r].rearrange("p t b s -> p (t b s)"))
                     for r in range(REP)]
                last = split_product(b_out[c // 2][:, 256 * (c % 2):256 * (c % 2) + 256], o)
                if c % 2:
                    last.then_inc(sm["wo_done"], 1)

            def output_layers(p, k, t, part):
                if t == 0:
                    pe.wait_ge(sm["x1_sum"], 2 * p + 2)
                    pe.wait_ge(sm["x1_l"], 2 * p + part + 1)
                    if part == 0 and k == 0:
                        pe.wait_ge(sm["fused_l"], C + 1)
                        pe.wait_ge(sm["a2r_l"], 1)
                if part == 0 and t == 1:
                    pe.wait_ge(sm["y_sb"], 2 * (2 * p + 1))
                for c in (2 * part, 2 * part + 1):
                    tok = slice(P * t, P * t + P)
                    for n, (a, b) in enumerate(((x1_hi, fw_hi), (x1_hi, fw_lo), (x1_lo, fw_hi))):
                        for h in range(2):
                            last = nc.tensor.matmul(b_out[h][:, 0:HALF], a[:, c, tok], b[:, c, HALF * h:HALF * h + HALF],
                                                    start=(c == 0 and n == 0), stop=(c == C - 1 and n == 2))
                if part == 1:
                    last.then_inc(sm["fin"], 1)

            def transpose_gated(p, t):
                pe.wait_ge(sm["gated"], 2 * p + t + 1)
                nc.tensor.transpose(b_mix[:, 0:P], gh[:, :], ident).then_inc(sm["ghT"], 1)

            def add_experts(p, t):
                pe.wait_ge(sm["ghT_l"], 2 * p + t + 1)
                for n, (a, b) in enumerate(((ghT_hi, bc_hi), (ghT_hi, bc_lo), (ghT_lo, bc_hi))):
                    nc.tensor.matmul(b_out0[:, ROUT:HALF], a[:, :], b[:, 0:OUT_A], start=False, stop=(n == 2),
                                     skip_group_check=True)
                    last = nc.tensor.matmul(b_out1[:, 0:HALF], a[:, :], b[:, OUT_A:D], start=False, stop=(n == 2),
                                            skip_group_check=True)
                last.then_inc(sm["fin2"], 1)

            def update_product(m):
                if m == 0:
                    pe.wait_ge(sm["prep_in"], 16 * 8)
                    pe.wait_ge(sm["scaled"], 3)
                if m >= 2:
                    pe.wait_ge(sm["wfull_sb"], m - 1)
                for e in range(2):
                    last = nc.tensor.matmul(b_out[m % 2][:, :], af_sb[:, e, P * m:P * m + P], bf_sb[:, e, :],
                                            start=(e == 0), stop=(e == 1))
                last.then_inc(sm["wprod"], 1)

            def fused_product(m):
                pe.wait_ge(sm["wfull_sb"], C)
                if m >= 2:
                    pe.wait_ge(sm["fused_sb"], 2 * (m - 2) + 1)
                for c in range(C):
                    left = w2_sb[:, c, P * m:P * m + P] if m < C else b2_sb[:, c, :]
                    last = nc.tensor.matmul(b_out[m % 2][:, :], left, wfull[:, c, :], start=(c == 0), stop=(c == C - 1))
                last.then_inc(sm["wprod"], 1)

            def body(i, k):
                a_next, a_after, w_now, w_tail = pair(k + 1), pair(k + 2), pair(k - 1), pair(k - 2)
                for s in range(SLOTS):
                    if pair(k):
                        scores(i, k, s)
                    late = pair(k - 1) if s < 2 else pair(k)
                    before = (i - 1, k - 1, SLOTS - 2 + s) if s < 2 else (i, k, s - 2)
                    if late:
                        probs_T(*before)
                    if s == 0:
                        if a_next:
                            project_q(i + 1, k + 1, 0, 0)
                            project_q(i + 1, k + 1, 0, 1)
                    if s == 1:
                        if w_tail:
                            transpose_gated(i - 2, 1)
                        if a_next:
                            project_kv(i + 1, k + 1, 0)
                        if late:
                            values(*before)
                        if w_tail:
                            add_experts(i - 2, 1)
                        if a_next:
                            if w_tail:
                                pe.wait_ge(sm["ghT_l"], 2 * (i - 2) + 2)
                            mix(i + 1, 1)
                        if k == 0:
                            update_product(0)
                            update_product(1)
                    if s == 2:
                        if w_now:
                            output_projection(i - 1, k - 1, 0)
                            output_projection(i - 1, k - 1, 1)
                        if k == 0:
                            update_product(2)
                            update_product(3)
                    if s == 3:
                        if w_now:
                            output_projection(i - 1, k - 1, 2)
                        if a_next:
                            transpose_qk(i + 1, 0)
                        if w_now:
                            output_projection(i - 1, k - 1, 3)
                        if k == 0:
                            fused_product(0)
                    if s == 4:
                        if a_next:
                            project_q(i + 1, k + 1, 1, 0)
                        if w_now:
                            output_layers(i - 1, k - 1, 0, 0)
                        if k == 0:
                            fused_product(1)
                    if s == 5:
                        if w_now:
                            output_layers(i - 1, k - 1, 0, 1)
                        if a_next:
                            project_q(i + 1, k + 1, 1, 1)
                        if k == 0:
                            fused_product(2)
                    if s == 6:
                        if a_next:
                            project_kv(i + 1, k + 1, 1)
                        if late:
                            values(*before)
                        if w_now:
                            transpose_gated(i - 1, 0)
                        if k == 0:
                            fused_product(3)
                    if s == 7:
                        if w_now:
                            add_experts(i - 1, 0)
                        if a_after:
                            if w_now:
                                pe.wait_ge(sm["ghT_l"], 2 * (i - 1) + 1)
                            mix(i + 2, 0)
                        if late:
                            values(*before)
                        if w_now:
                            output_layers(i - 1, k - 1, 1, 0)
                            output_layers(i - 1, k - 1, 1, 1)
                        if k == 0:
                            fused_product(4)
                    if late and s not in (1, 6, 7):
                        values(*before)
                    if s == 7 and a_next:
                        transpose_qk(i + 1, 1)

            pe.wait_ge(sm["const_in"], 16)
            pe.wait_ge(sm["wqkv_l"], C)
            steps(pe, body)


_OUT = (NSEQ, S, D)


def kernel(x, itok_B_0_15, itok_B_0_7, L0_cond_weights, L0_attn_Wq, L0_attn_Wk, L0_attn_Wv, L0_attn_Wo,
           L0_cond2_W, L0_cond2_Wr, L0_cond2_A, L0_cond2_B, L0_ffn_W, L0_ffn_bias, L0_ffn_A, L0_ffn_Bf,
           L0_ffn_coeffs, L0_ffn_scales):
    import concourse.bacc as _bacc
    from concourse.bass_utils import run_bass_kernel_spmd as _run

    def chunked(w, n=C):
        return np.ascontiguousarray(np.asarray(w).reshape(n, P, -1).transpose(1, 0, 2))

    x = np.ascontiguousarray(x)
    q_rows = np.asarray(L0_attn_Wq).reshape(HKV, REP, HD, D).transpose(1, 0, 2, 3).reshape(D, D)
    qkv_rows = np.concatenate([q_rows, np.asarray(L0_attn_Wk), np.asarray(L0_attn_Wv)], 0)
    o_cols = np.asarray(L0_attn_Wo).reshape(D, HKV, REP, HD).transpose(2, 1, 3, 0).reshape(D, D)
    a2 = np.asarray(L0_cond2_A).reshape(E2 * R2, D)
    a2r = np.concatenate([a2, np.asarray(L0_cond2_Wr)], 0).T
    b2 = np.asarray(L0_cond2_B).transpose(1, 0, 2).reshape(D, E2 * R2)
    bf = np.asarray(L0_ffn_Bf).transpose(0, 2, 1).reshape(EF * 16, D)
    lang = np.asarray(itok_B_0_7).reshape(PAIRS, 2, SEQ_PER_TILE, 1)
    lang = np.broadcast_to(lang, (PAIRS, 2, SEQ_PER_TILE, S)).reshape(PAIRS, 2, P).transpose(0, 2, 1)

    inv = (1.0 / 10000.0 ** (np.arange(0, HD, 2, dtype=np.float32) / np.float32(HD))).astype(np.float32)
    ang = np.outer(np.arange(S, dtype=np.float32), inv)
    c, s_ = np.cos(ang), np.sin(ang)
    consts = np.zeros((P, K_ALL), np.float32)
    consts[:, K_COS:K_COS + HD] = np.tile(np.concatenate([c, c], 1), (SEQ_PER_TILE, 1))
    consts[:, K_SIN:K_SIN + HD] = np.tile(np.concatenate([-s_, s_], 1), (SEQ_PER_TILE, 1))
    consts[:, K_MASK:K_MASK + S] = np.tile(np.triu(np.full((S, S), MASKED, np.float32), 1), (REP, 1))
    consts[:, K_IOTA:K_IOTA + E2] = np.arange(E2)
    consts[:, K_ID:K_ID + P] = np.eye(P)

    given = {
        "x": x,
        "xT": np.ascontiguousarray(x.reshape(NSEQ * S, D).T),
        "cond": np.ascontiguousarray(itok_B_0_15),
        "lang": np.ascontiguousarray(lang),
        "wcond": np.ascontiguousarray(L0_cond_weights),
        "wqkv": chunked(qkv_rows.T),
        "wo": chunked(o_cols),
        "w2": chunked(L0_cond2_W),
        "a2r": chunked(a2r),
        "b2": chunked(b2),
        "wf": chunked(np.asarray(L0_ffn_W).T),
        "af": chunked(np.asarray(L0_ffn_A).reshape(EF * 16, D), 2),
        "bf": chunked(bf, 2),
        "coeffs": np.ascontiguousarray(np.repeat(np.asarray(L0_ffn_coeffs), 16).reshape(2, P).T),
        "scales": np.ascontiguousarray(np.repeat(np.asarray(L0_ffn_scales), 16).reshape(2, P).T),
        "bias": np.ascontiguousarray(L0_ffn_bias),
        "consts": consts,
    }
    nc = _bacc.Bacc("TRN2", target_bir_lowering=False, num_devices=1)
    arrays, args = {}, {}
    for name, a in given.items():
        arrays[f"{name}_dram"] = a
        args[name] = nc.dram_tensor(f"{name}_dram", a.shape, mybir.dt.from_np(a.dtype), kind="ExternalInput").ap()
    out = nc.dram_tensor("out_dram", _OUT, F32, kind="ExternalOutput").ap()
    program(nc, out=out, **args)
    r = _run(nc, [arrays], core_ids=[0])
    return r.results[0]["out_dram"]
```

```python
from contextlib import ExitStack

import concourse.bass as bass
from concourse import mybir
import numpy as np

P = 128
NSEQ, S, D = 64, 32, 512
SEQ_PER_TILE = P // S
TILES = NSEQ // SEQ_PER_TILE
PAIRS = TILES // 2
SLOTS = 2 * SEQ_PER_TILE
HKV, REP, HD = 8, 4, 16
C = D // P
QKV = D + 2 * HKV * HD
E2, R2 = 8, 16
EF = 16
ROUT = E2 * R2 + E2
FW = ROUT + D
HALF = FW // 2
OUT_A = HALF - ROUT
LANG_BIAS = 5.0
SCALING = 2.0
MASKED = -1.0e30
CHOOSE_STEPS, GATE_STEPS = 7, 11

F32 = mybir.dt.float32
F32R = mybir.dt.float32r
I32 = mybir.dt.int32
U32 = mybir.dt.uint32
ALU = mybir.AluOpType
ACT = mybir.ActivationFunctionType
AX = mybir.AxisListType

K_COS, K_SIN, K_MASK, K_IOTA, K_GROUP, K_ID = np.cumsum([0, HD, HD, S, E2, HKV]).tolist()
K_ALL = K_ID + P

FUSED_SLOTS = [1, 2, 3, 5, 7]
FUSED_SPLITS = [(0, 2), (0, 3), (0, 4), (0, 7), (1, 0)]
A2R_SLOT = 1
LOOP_FROM, LOOP_TO = 2, PAIRS - 2


def program(nc, x, xT, cond, lang, wcond, wqkv, wo, w2b2, a2r, wf, afbf, cs, bias, consts, out):
    x_t = x.rearrange("(n b) c f -> n (b c) f", b=SEQ_PER_TILE)
    out_t = out.rearrange("(n b) c f -> n (b c) f", b=SEQ_PER_TILE)
    xT_p = xT.rearrange("(c p) n -> p c n", p=P)

    ctx = ExitStack()
    with ctx:
        def sb(name, shape, dt=F32):
            return ctx.enter_context(nc.sbuf_tensor(name, shape, dt))

        def pb(name, shape):
            return ctx.enter_context(nc.psum_tensor(name, shape, F32))

        def sem(name):
            return ctx.enter_context(nc.semaphore(name))

        def pair_of(name, shape):
            return sb(name + "_hi", shape, F32R), sb(name + "_lo", shape, F32R)

        const = sb("const", [P, K_ALL])
        cos = const[:, K_COS:K_COS + HD]
        sin = const[:, K_SIN:K_SIN + HD]
        mask = const[:, K_MASK:K_MASK + S]
        iota = const[:, K_IOTA:K_IOTA + E2]
        group = const[:, K_GROUP:K_GROUP + HKV]
        ident = const[:, K_ID:K_ID + P]
        cond_sb = sb("cond_sb", [1, NSEQ], I32)
        wqkv_hi, wqkv_lo = pair_of("wqkv", [P, C, QKV])
        wqkv_raw = sb("wqkv_raw", [P, C, QKV])
        wo_hi, wo_lo = pair_of("wo", [P, C, D])
        wo_raw = sb("wo_raw", [P, C, D])
        w2b2_hi, w2b2_lo = pair_of("w2b2", [P, C, D + E2 * R2])
        w2b2_raw = wqkv_raw[:, :, 0:D + E2 * R2]
        wfull = sb("wfull", [P, C, D])
        wfull_hi, wfull_lo = pair_of("wfull", [P, C, D])
        a2r_sb = sb("a2r_sb", [P, C, ROUT])
        afbf_sb = sb("afbf_sb", [P, 4, D])
        af_sb, bf_sb = afbf_sb[:, 0:2], afbf_sb[:, 2:4]
        cw = sb("cw", [P, 3, 2])
        bias_sb = sb("bias_sb", [P, D])
        fused = wfull[:, 2:4, :]
        fw_hi, fw_lo = pair_of("fw", [P, C, FW])
        bc_hi, bc_lo = pair_of("bc", [P, D])
        xt = sb("xt", [P, 2, D])
        wbd = sb("wbd", [P, 2, P])
        hT_hi, hT_lo = pair_of("hT", [P, 2, C, P])
        rope_cos = sb("rope_cos", [P, 5, P])
        rope_sin = sb("rope_sin", [P, 5, P])
        qk = sb("qk", [P, 5, P])
        vst = sb("vst", [P, 2, P])
        QT_hi, QT_lo = pair_of("QT", [P, 2, SEQ_PER_TILE, REP, S])
        kT_hi = sb("kT_hi", [P, 2, P], F32R)
        kT_lo = sb("kT_lo", [P, 2, P])
        Kbd_hi, Kbd_lo = pair_of("Kbd", [P, 2, HKV, P])
        Vbd = sb("Vbd", [P, 2, SEQ_PER_TILE, 2, 64])
        v_dram = nc.dram_tensor("v_scratch", [2, P, P], F32).ap()
        att = sb("att", [P, 4, HKV, S])
        rowmax = sb("rowmax", [P, 2, HKV])
        rowsum = sb("rowsum", [P, 2, HKV])
        rowinv = sb("rowinv", [P, 2, HKV])
        PTs = wqkv_raw[:, 0, 0:4 * P].rearrange("p (a h n) -> p a h n", a=2, h=2)
        oT_hi, oT_lo = pair_of("oT", [P, REP, 2, SEQ_PER_TILE, S])
        xres = wfull[:, 0:2, :].rearrange("p a (b n) -> p (a b) n", b=2)
        y = afbf_sb[:, 0:2, :]
        x1 = afbf_sb[:, 2:4, :].rearrange("p a (b n) -> p (a b) n", b=2)
        x1_hi, x1_lo = [wfull_hi[:, 2 * a:2 * a + 2, :].rearrange("p a (b n) -> p (a b) n", b=2) for a in range(2)]
        x1_hi_last, x1_lo_last = [wfull_lo[:, 2 * a:2 * a + 2, :].rearrange("p a (b n) -> p (a b) n", b=2)
                                  for a in range(2)]
        ids = sb("ids", [P, 2], I32)
        ids_last = sb("ids_last", [P, 2], I32)
        lbias = sb("lbias", [P, E2])
        logits = sb("logits", [P, E2])
        top8 = sb("top8", [P, E2])
        idx8 = sb("idx8", [P, E2], U32)
        idxf = sb("idxf", [P, 2])
        gs = sb("gs", [P, 8])
        first = sb("first", [P, E2])
        second = sb("second", [P, E2])
        gates = sb("gates", [P, E2])
        gh = sb("gh", [P, E2 * R2])
        ghT_hi, ghT_lo = pair_of("ghT", [P, P])

        b_mix = pb("b_mix", [P, 512])
        b_qkv = pb("b_qkv", [P, 1024])
        b_out0 = pb("b_out0", [P, 512])
        b_out1 = pb("b_out1", [P, 512])
        b_s = pb("b_s", [P, 512])
        b_pt = pb("b_pt", [P, 512])
        b_o = pb("b_o", [P, 512])
        b_out = [b_out0, b_out1]

        def product_banks(k):
            return [b_qkv[:, 0:512], b_qkv[:, 512:1024]] if k == PAIRS - 1 else b_out

        def x1_parts(k):
            return (x1_hi, x1_lo) if k < PAIRS - 1 else (x1_hi_last, x1_lo_last)

        def output_banks(k, t):
            return product_banks(k) if t == 0 else b_out

        def gated_columns(k, t):
            return b_qkv[:, QKV:QKV + P] if t == 0 and k < PAIRS - 2 else b_mix[:, 0:P]

        names = """const_in cond_in update_in wf_in w2_in wo_in a2r_in bias_in zeroed wqkv_h wqkv_l wo_h wo_l
            scaled wprod wfull_sb wfull_h wfull_l w2b2_h w2b2_l fused_sb fused_h fused_l a2r_h a2r_l
            mixed hT_h hT_l q_done kv_done rope_terms roped v_out qT kT qT_h qT_l kT_h kT_l kbd_l
            scored masked maxed shifted expd summed inverted normed pT pT_sb pv oT_h oT_l
            wo_done x1_sum x1_h x1_l fin gate_steps gate_exp gated ghT ghT_h ghT_l fin2 y_sb
            xres_in ids_in ids_last_in sp_passed"""
        sm = {n: sem(n) for n in names.split()}
        wqkv_in = [sem(f"wqkv_in{c}") for c in range(C)]
        x_in = [sem(f"x_in{t}") for t in range(2)]
        w_in = [sem(f"w_in{t}") for t in range(2)]
        v_scr = [sem(f"v_scr{t}") for t in range(2)]
        v_in = [sem(f"v_in{t}") for t in range(2)]
        stored = [sem(f"stored{t}") for t in range(2)]

        def steps(engine, body, last=PAIRS - 1):
            for i in range(-2, LOOP_FROM):
                body(i, i)
            with engine.Fori(LOOP_FROM, LOOP_TO) as i:
                body(i, LOOP_FROM)
            for i in range(LOOP_TO, last + 1):
                body(i, i)

        def pair(k):
            return 0 <= k < PAIRS

        block = ctx.enter_context(nc.Block())

        @block.sync
        def _(sp):
            sp.dma_start(cond_sb[0:1, :], cond.rearrange("(a n) -> a n", a=1)).then_inc(sm["cond_in"], 16)
            sp.dma_start(const[:, :], consts).then_inc(sm["const_in"], 16)
            for t in range(2):
                sp.dma_start(xt[:, t, :], x_t[t]).then_inc(x_in[t], 16)
            sp.wait_ge(sm["cond_in"], 16)
            sp.wait_ge(sm["zeroed"], 1)

            def settled():
                sp.wait_ge(sm["cond_in"], 16)

            def load_tokens(n, t):
                settled()
                sp.dma_start(xt[:, t, :], x_t[2 * n + t]).then_inc(x_in[t], 16)

            def load_mixing(n, t):
                for b in range(SEQ_PER_TILE):
                    at = 8 * n + 4 * t + b
                    which = sp.value_load(cond_sb[0:1, bass.ds(at, 1)], min_val=0, max_val=15)
                    sp.dma_start(wbd[S * b:S * b + S, t, S * b:S * b + S],
                                 wcond[bass.ds(which, 1)].rearrange("a c d -> (a c) d")).then_inc(w_in[t], 16)

            def spread_v(k, t):
                if k == 0 and t == 0:
                    sp.wait_ge(sm["zeroed"], 2)
                src = v_dram[t].rearrange("(k b) (h g d) -> k (b h) g d", b=SEQ_PER_TILE, h=2, g=4)
                for g in range(4):
                    dst = Vbd[S * g:S * g + S, t, :, :, HD * g:HD * g + HD]
                    sp.dma_start(dst.rearrange("p b h d -> p (b h) d"), src[:, :, g, :]).then_inc(v_in[t], 16)

            def passed():
                sp.sem_inc(sm["sp_passed"], 1)

            def v_to_dram(n, k, t):
                sp.wait_ge(sm["v_out"], 2 * n + t + 1)
                if k > 0:
                    passed()
                    sp.wait_ge(v_in[t], 64 * n)
                sp.dma_start(v_dram[t].rearrange("(k b) c -> b k c", b=SEQ_PER_TILE),
                             vst[:, t, :]).then_inc(v_scr[t], 16)

            def body(i, k):
                if pair(k + 2):
                    if k > -2:
                        sp.wait_ge(sm["mixed"], 2 * (i + 1) + 1)
                        load_tokens(i + 2, 0)
                    load_mixing(i + 2, 0)
                if k == 1:
                    sp.dma_start(ids_last[:, :], lang[PAIRS - 1]).then_inc(sm["ids_last_in"], 16)
                if pair(k - 1) and k < PAIRS:
                    if k > 1:
                        sp.wait_ge(sm["gated"], 2 * (i - 2) + 2)
                    settled()
                    sp.dma_start(ids[:, :], lang[i - 1]).then_inc(sm["ids_in"], 16)
                if pair(k):
                    sp.wait_ge(v_scr[1], 16 * (i + 1))
                    if k > 0:
                        passed()
                        sp.wait_ge(sm["pv"], 8 * i)
                    spread_v(k, 1)
                if pair(k - 2):
                    sp.wait_ge(sm["y_sb"], 2 * (2 * (i - 2) + 2))
                    settled()
                    sp.dma_start(out_t[2 * (i - 2) + 1], y[:, 1, :]).then_inc(stored[1], 16)
                if pair(k + 1):
                    v_to_dram(i + 1, k + 1, 0)
                if pair(k + 2):
                    if k > -2:
                        sp.wait_ge(sm["mixed"], 2 * (i + 1) + 2)
                        load_tokens(i + 2, 1)
                    load_mixing(i + 2, 1)
                if pair(k):
                    if k == 0:
                        sp.wait_ge(sm["wfull_l"], C)
                    if k > 0:
                        sp.wait_ge(sm["x1_sum"], 2 * (i - 1) + 2)
                    settled()
                    sp.dma_start(xres[:, :, :], xT_p[:, :, bass.ds(i * (2 * P), 2 * P)]).then_inc(sm["xres_in"], 16)
                if pair(k + 1):
                    sp.wait_ge(v_scr[0], 16 * (i + 2))
                    if k >= 0:
                        passed()
                        sp.wait_ge(sm["pv"], 8 * i + 4)
                    spread_v(k + 1, 0)
                    v_to_dram(i + 1, k + 1, 1)
                if pair(k - 1):
                    sp.wait_ge(sm["y_sb"], 2 * (2 * (i - 1) + 1))
                    settled()
                    sp.dma_start(out_t[2 * (i - 1)], y[:, 0, :]).then_inc(stored[0], 16)

            for t in range(2):
                sp.sem_inc(stored[t], 16)
            steps(sp, body, PAIRS + 1)
            for t in range(2):
                sp.wait_ge(stored[t], 16 * (PAIRS + 1))
                sp.wait_ge(v_scr[t], 16 * PAIRS)

        @block.gpsimd
        def _(pool):
            nc.gpsimd.memset(wbd[:, :, :], 0.0).then_inc(sm["zeroed"], 1)
            nc.gpsimd.memset(Vbd[:, :, :, :, :], 0.0).then_inc(sm["zeroed"], 1)

            def subtract(dst, full, high, signal):
                nc.gpsimd.tensor_tensor(dst, full, high.bitcast(F32), ALU.subtract).then_inc(signal, 1)

            def shift(i, s):
                pool.wait_ge(sm["maxed"], 8 * i + s + 1)
                m = rowmax[:, s % 2, :].unsqueeze(2).broadcast_to([P, HKV, S])
                nc.gpsimd.tensor_tensor(att[:, s % 4], att[:, s % 4], m, ALU.subtract).then_inc(sm["shifted"], 1)

            def normalise(i, s):
                pool.wait_ge(sm["inverted"], 8 * i + s + 1)
                r = rowinv[:, s % 2, :].unsqueeze(2).broadcast_to([P, HKV, S])
                nc.gpsimd.tensor_tensor(att[:, s % 4], att[:, s % 4], r, ALU.mult).then_inc(sm["normed"], 1)

            def rope_sum(n, t):
                pool.wait_ge(sm["rope_terms"], 3 * (2 * n + t) + 3)
                nc.gpsimd.tensor_tensor(qk[:, :, :], rope_cos[:, :, :], rope_sin[:, :, :],
                                        ALU.add).then_inc(sm["roped"], 1)

            def k_blocks_low(n, t, h):
                if h == 0:
                    pool.wait_ge(sm["kT_l"], 2 * n + t + 1)
                heads = slice(h * HKV // 2, (h + 1) * HKV // 2)
                shape = [P, HKV // 2, P]
                nc.gpsimd.tensor_tensor(Kbd_lo[:, t, heads, :], kT_lo[:, t, :].unsqueeze(1).broadcast_to(shape),
                                        group[:, heads].unsqueeze(2).broadcast_to(shape),
                                        ALU.mult).then_inc(sm["kbd_l"], 1)

            def x1_low(p, h):
                pool.wait_ge(sm["x1_h"], 2 * p + h + 1)
                subtract(x1_lo[:, 2 * h:2 * h + 2, :], x1[:, 2 * h:2 * h + 2, :],
                         x1_hi[:, 2 * h:2 * h + 2, :], sm["x1_l"])

            def fused_low(m):
                pool.wait_ge(sm["fused_h"], m + 1)
                if m < C:
                    subtract(fw_lo[:, m, ROUT:FW], fused[:, m % 2, :], fw_hi[:, m, ROUT:FW], sm["fused_l"])
                else:
                    subtract(bc_lo[:, :], fused[:, m % 2, :], bc_hi[:, :], sm["fused_l"])

            def body(i, k):
                for s in range(SLOTS):
                    if s == 0 and pair(k - 1):
                        normalise(i - 1, SLOTS - 1)
                    if s == 6 and pair(k):
                        normalise(i, s - 1)
                    if s == 7 and k >= 0 and pair(k + 1):
                        rope_sum(i + 1, 1)
                    if pair(k):
                        shift(i, s)
                    if s not in (0, 6) and pair(k):
                        normalise(i, s - 1)
                    if s in (0, 1) and pair(k):
                        k_blocks_low(i, 1, s)
                    if s in (5, 6) and pair(k + 1):
                        k_blocks_low(i + 1, 0, s - 5)
                    if (k, s) == (-1, 7):
                        for c in range(C // 2, C):
                            pool.wait_ge(sm["w2b2_h"], c + 1)
                            subtract(w2b2_lo[:, c, :], w2b2_raw[:, c, :], w2b2_hi[:, c, :], sm["w2b2_l"])
                        for c in range(C):
                            pool.wait_ge(sm["wo_h"], c + 1)
                            subtract(wo_lo[:, c, :], wo_raw[:, c, :], wo_hi[:, c, :], sm["wo_l"])
                    if s == 2 and k >= 0 and pair(k + 1):
                        rope_sum(i + 1, 0)
                    if s == 3 and pair(k - 1) and k < PAIRS - 1:
                        x1_low(i - 1, 0)
                        x1_low(i - 1, 1)
                    if k == 0 and s == A2R_SLOT:
                        pool.wait_ge(sm["a2r_h"], 1)
                        subtract(fw_lo[:, :, 0:ROUT], a2r_sb[:, :, :], fw_hi[:, :, 0:ROUT], sm["a2r_l"])
                    if (k, s) in FUSED_SPLITS:
                        fused_low(FUSED_SPLITS.index((k, s)))

            steps(pool, body)
            normalise(PAIRS - 1, SLOTS - 1)

        @block.scalar
        def _(act):
            for c in range(C):
                act.dma_start(wqkv_raw[:, c, :], wqkv[:, c, :]).then_inc(wqkv_in[c], 16)
            for c in range(C):
                act.wait_ge(wqkv_in[c], 16)
                nc.scalar.copy(wqkv_hi[:, c, :], wqkv_raw[:, c, :]).then_inc(sm["wqkv_h"], 1)
            for dst, src in ((afbf_sb[:, :, :], afbf), (cw[:, 0:2, :], cs)):
                act.dma_start(dst, src).then_inc(sm["update_in"], 16)

            def load_later_weights():
                act.dma_start(wfull[:, :, :], wf).then_inc(sm["wf_in"], 16)
                act.wait_ge(sm["wqkv_l"], C)
                act.dma_start(w2b2_raw[:, :, :], w2b2).then_inc(sm["w2_in"], 16)
                act.dma_start(wo_raw[:, :, :], wo).then_inc(sm["wo_in"], 16)
                act.dma_start(a2r_sb[:, :, :], a2r).then_inc(sm["a2r_in"], 16)
                act.dma_start(bias_sb[:, :], bias.rearrange("(a n) -> a n", a=1).broadcast_to([P, D])
                              ).then_inc(sm["bias_in"], 16)

            def mix_high(n, t):
                act.wait_ge(sm["mixed"], 2 * n + t + 1)
                nc.scalar.copy(hT_hi[:, t].rearrange("p c n -> p (c n)"), b_mix[:, :]).then_inc(sm["hT_h"], 1)

            def value_copy(n, k, t):
                act.wait_ge(sm["kv_done"], 2 * n + t + 1)
                if k > 0:
                    act.wait_ge(v_scr[t], 16 * n)
                nc.scalar.copy(vst[:, t, :], b_qkv[:, D + P:D + 2 * P]).then_inc(sm["v_out"], 1)

            def q_high(n, t):
                act.wait_ge(sm["qT"], 2 * n + t + 1)
                src = b_qkv[:, 0:D].rearrange("p (r b s) -> p b r s", r=REP, b=SEQ_PER_TILE)
                nc.scalar.copy(QT_hi[:, t], src).then_inc(sm["qT_h"], 1)

            def k_high(n, t):
                act.wait_ge(sm["kT"], 2 * n + t + 1)
                for g in range(HKV):
                    nc.scalar.activation(Kbd_hi[:, t, g, :], b_qkv[:, D:D + P], ACT.Identity, scale=group[:, g:g + 1])
                nc.scalar.copy(kT_hi[:, t, :], b_qkv[:, D:D + P]).then_inc(sm["kT_h"], 1)

            def probs_T_copy(i, k, s):
                act.wait_ge(sm["pT"], 8 * i + s + 1)
                if k > 0 or s >= 2:
                    act.wait_ge(sm["pv"], 8 * i + s - 1)
                nc.scalar.copy(PTs[:, s % 2].rearrange("p h n -> p (h n)"), b_pt[:, 0:2 * P]).then_inc(sm["pT_sb"], 1)

            def exps(i, s):
                act.wait_ge(sm["shifted"], 8 * i + s + 1)
                nc.scalar.activation(att[:, s % 4], att[:, s % 4], ACT.Exp,
                                     scale=float(HD) ** -0.5).then_inc(sm["expd"], 1)

            def o_high(i, t):
                act.wait_ge(sm["pv"], 8 * i + 4 * t + 4)
                src = b_o[:, :].rearrange("p (b r s) -> p r b s", b=SEQ_PER_TILE, r=REP)
                nc.scalar.copy(oT_hi[:, :, t], src).then_inc(sm["oT_h"], 1)

            def x1_high(p, k, h):
                act.wait_ge(sm["x1_sum"], 2 * p + h + 1)
                nc.scalar.copy(x1_parts(k)[0][:, 2 * h:2 * h + 2, :], x1[:, 2 * h:2 * h + 2, :]).then_inc(sm["x1_h"], 1)

            def gate_exp(p, t):
                act.wait_ge(sm["gate_steps"], GATE_STEPS * (2 * p + t) + 4)
                nc.scalar.activation(gs[:, 1:2], gs[:, 0:1], ACT.Exp).then_inc(sm["gate_exp"], 1)

            def gh_high(p, k, t):
                act.wait_ge(sm["ghT"], 2 * p + t + 1)
                nc.scalar.copy(ghT_hi[:, :], gated_columns(k, t)).then_inc(sm["ghT_h"], 1)

            def full_high(m):
                act.wait_ge(sm["wfull_sb"], m + 1)
                nc.scalar.copy(wfull_hi[:, m, :], wfull[:, m, :]).then_inc(sm["wfull_h"], 1)

            def fused_high(m):
                act.wait_ge(sm["fused_sb"], 2 * m + 2 if m < C else 2 * C + 1)
                dst = fw_hi[:, m, ROUT:FW] if m < C else bc_hi[:, :]
                nc.scalar.copy(dst, fused[:, m % 2, :]).then_inc(sm["fused_h"], 1)

            def body(i, k):
                for s in range(SLOTS):
                    if s == 6 and pair(k + 1):
                        value_copy(i + 1, k + 1, 1)
                    if s == 6 and pair(k):
                        o_high(i, 0)
                    if s == 6 and pair(k - 1) and k < PAIRS - 1:
                        gh_high(i - 1, k - 1, 0)
                    if s < 2:
                        if pair(k - 1):
                            probs_T_copy(i - 1, k - 1, SLOTS - 2 + s)
                    elif pair(k):
                        probs_T_copy(i, k, s - 2)
                    if s == 0 and k > 0 and pair(k + 1):
                        mix_high(i + 1, 1)
                    if s == 0 and k > 0 and pair(k):
                        k_high(i, 1)
                    if s == 1 and pair(k - 2):
                        gh_high(i - 2, k - 2, 1)
                    if s == 2 and k == -1:
                        mix_high(0, 1)
                    if s == 3 and pair(k + 1):
                        q_high(i + 1, 0)
                    if s == 3 and pair(k - 1):
                        x1_high(i - 1, k - 1, 0)
                    if (k, s) == (0, 0):
                        mix_high(1, 1)
                    if s == 1 and pair(k):
                        exps(i, 0)
                    if s == 1 and pair(k - 1):
                        o_high(i - 1, 1)
                    if pair(k) and s > 0:
                        exps(i, s)
                    if s == 1 and pair(k + 1):
                        value_copy(i + 1, k + 1, 0)
                    if s == (3 if k < PAIRS - 1 else 5) and pair(k - 1):
                        x1_high(i - 1, k - 1, 1)
                    if s == 4 and k >= 0 and pair(k + 1):
                        k_high(i + 1, 0)
                    if s == (5 if k < PAIRS - 1 else 7) and pair(k - 1):
                        gate_exp(i - 1, 0)
                    if s == 6 and pair(k + 2):
                        mix_high(i + 2, 0)
                    if (k, s) == (-1, 6):
                        nc.scalar.copy(w2b2_hi[:, C - 1, :], w2b2_raw[:, C - 1, :]).then_inc(sm["w2b2_h"], 1)
                        act.wait_ge(sm["wo_in"], 16)
                        for c in range(C):
                            nc.scalar.copy(wo_hi[:, c, :], wo_raw[:, c, :]).then_inc(sm["wo_h"], 1)
                    if s == 7 and k == -2:
                        load_later_weights()
                    if s == 7 and pair(k - 1) and k < PAIRS - 1:
                        gate_exp(i - 1, 1)
                    if s == 7 and pair(k + 1):
                        q_high(i + 1, 1)
                    if s == 7 and k == -1:
                        k_high(i + 1, 1)
                    if k == -1 and s == 3:
                        k_high(0, 0)
                        full_high(0)
                        full_high(1)
                    if k == -1 and s == 4:
                        act.wait_ge(sm["w2_in"], 16)
                        for c in range(C - 1):
                            nc.scalar.copy(w2b2_hi[:, c, :], w2b2_raw[:, c, :]).then_inc(sm["w2b2_h"], 1)
                    if k == -1 and s == 7:
                        full_high(2)
                        full_high(3)
                    if k == 0 and s == A2R_SLOT:
                        act.wait_ge(sm["a2r_in"], 16)
                        nc.scalar.copy(fw_hi[:, :, 0:ROUT], a2r_sb[:, :, :]).then_inc(sm["a2r_h"], 1)
                    if (k, s) in FUSED_SPLITS:
                        fused_high(FUSED_SPLITS.index((k, s)))

            steps(act, body)
            p, q = PAIRS - 2, PAIRS - 1
            probs_T_copy(q, q, 6)
            gh_high(p, p, 0)
            probs_T_copy(q, q, 7)
            o_high(q, 1)
            gate_exp(p, 1)
            x1_high(q, q, 0)
            gh_high(p, p, 1)
            x1_high(q, q, 1)
            gate_exp(q, 0)
            gh_high(q, q, 0)
            gate_exp(q, 1)
            gh_high(q, q, 1)

        @block.vector
        def _(dve):
            def low(dst, full, high, signal):
                nc.vector.tensor_tensor(dst, full, high.bitcast(F32), ALU.subtract).then_inc(signal, 1)

            def mix_low(n, t):
                dve.wait_ge(sm["hT_h"], 2 * n + t + 1)
                low(hT_lo[:, t].rearrange("p c n -> p (c n)"), b_mix[:, :],
                    hT_hi[:, t].rearrange("p c n -> p (c n)"), sm["hT_l"])

            def rope_products(n, k, t):
                if k == 0 and t == 0:
                    dve.wait_ge(sm["const_in"], 16)
                dve.wait_ge(sm["q_done"], 2 * n + t + 1)
                dve.wait_ge(sm["v_out"], 2 * n + t + 1)
                if k > 0 or t > 0:
                    dve.wait_ge(sm["roped"], 2 * n + t)
                heads = (D + P) // HD
                q = b_qkv[:, 0:D + P].rearrange("p (h d) -> p h d", d=HD)
                c_out = rope_cos[:, :, :].rearrange("p c (h d) -> p (c h) d", d=HD)
                s_out = rope_sin[:, :, :].rearrange("p c (h d) -> p (c h) d", d=HD)
                half = HD // 2
                nc.vector.tensor_tensor(c_out, q, cos.unsqueeze(1).broadcast_to([P, heads, HD]),
                                        ALU.mult).then_inc(sm["rope_terms"], 1)
                for lo, hi in ((0, half), (half, 0)):
                    nc.vector.tensor_tensor(s_out[:, :, lo:lo + half], q[:, :, hi:hi + half],
                                            sin[:, lo:lo + half].unsqueeze(1).broadcast_to([P, heads, half]),
                                            ALU.mult).then_inc(sm["rope_terms"], 1)
                if k == 0:
                    dve.wait_ge(sm["rope_terms"], 3 * t + 3)
                    nc.vector.tensor_tensor(qk[:, :, :], rope_cos[:, :, :], rope_sin[:, :, :],
                                            ALU.add).then_inc(sm["roped"], 1)

            def q_low(n, t):
                dve.wait_ge(sm["qT_h"], 2 * n + t + 1)
                src = b_qkv[:, 0:D].rearrange("p (r b s) -> p b r s", r=REP, b=SEQ_PER_TILE)
                low(QT_lo[:, t], src, QT_hi[:, t], sm["qT_l"])

            def k_low(n, t):
                dve.wait_ge(sm["kT_h"], 2 * n + t + 1)
                low(kT_lo[:, t, :], b_qkv[:, D:D + P], kT_hi[:, t, :], sm["kT_l"])

            def mask_and_max(i, k, s):
                dve.wait_ge(sm["scored"], 8 * i + s + 1)
                m = mask.unsqueeze(1).broadcast_to([P, HKV, S])
                nc.vector.tensor_tensor(att[:, s % 4], b_s[:, 0:HKV * S].rearrange("p (g k) -> p g k", g=HKV), m,
                                        ALU.add).then_inc(sm["masked"], 1)
                dve.wait_ge(sm["masked"], 8 * i + s + 1)
                nc.vector.tensor_reduce(rowmax[:, s % 2, :], att[:, s % 4], AX.X, ALU.max).then_inc(sm["maxed"], 1)

            def row_sums(i, s):
                dve.wait_ge(sm["expd"], 8 * i + s + 1)
                nc.vector.tensor_reduce(rowsum[:, s % 2, :], att[:, s % 4], AX.X, ALU.add).then_inc(sm["summed"], 1)
                dve.wait_ge(sm["summed"], 8 * i + s + 1)
                nc.vector.reciprocal(rowinv[:, s % 2, :], rowsum[:, s % 2, :]).then_inc(sm["inverted"], 1)

            def o_low(i, t):
                dve.wait_ge(sm["oT_h"], 2 * i + t + 1)
                src = b_o[:, :].rearrange("p (b r s) -> p r b s", b=SEQ_PER_TILE, r=REP)
                low(oT_lo[:, :, t], src, oT_hi[:, :, t], sm["oT_l"])

            def add_residual(p, k, h):
                dve.wait_ge(sm["wo_done"], 2 * p + h + 1)
                dve.wait_ge(sm["xres_in"], 16 * (p + 1))
                nc.vector.tensor_tensor(x1[:, 2 * h:2 * h + 2, :],
                                        product_banks(k)[h].rearrange("p (c n) -> p c n", c=2),
                                        xres[:, 2 * h:2 * h + 2, :], ALU.add).then_inc(sm["x1_sum"], 1)

            def late_x1_low(p, h):
                chunks = slice(2 * h, 2 * h + 2)
                hi, lo = x1_parts(p)
                dve.wait_ge(sm["x1_h"], 2 * p + h + 1)
                low(lo[:, chunks, :], x1[:, chunks, :], hi[:, chunks, :], sm["x1_l"])

            def gate_counters(start):
                done = [start]

                def count(instruction):
                    done[0] = done[0] + 1
                    instruction.then_inc(sm["gate_steps"], 1)

                def step(instruction):
                    count(instruction)
                    dve.wait_ge(sm["gate_steps"], done[0])

                return count, step

            def choose_experts(p, k, t):
                low_bank = output_banks(k, t)[0]
                count, step = gate_counters(GATE_STEPS * (2 * p + t))
                if k < PAIRS - 1:
                    dve.wait_ge(sm["ids_in"], 16 * (p + 1))
                else:
                    dve.wait_ge(sm["ids_last_in"], 16)
                language = (ids if k < PAIRS - 1 else ids_last)[:, t:t + 1]
                step(nc.vector.tensor_scalar(lbias[:, :], iota, language, LANG_BIAS, ALU.is_equal, ALU.mult))
                dve.wait_ge(sm["fin"], 2 * p + t + 1)
                step(nc.vector.tensor_tensor(logits[:, :], low_bank[:, E2 * R2:ROUT], lbias[:, :], ALU.add))
                nc.vector.tensor_copy(gs[:, 6:7], logits[:, 0:1])
                step(nc.vector.max(top8[:, :], logits[:, :]))
                count(nc.vector.tensor_tensor(gs[:, 0:1], top8[:, 1:2], top8[:, 0:1], ALU.subtract))
                step(nc.vector.max_index(idx8[:, :], top8[:, :], logits[:, :]))
                step(nc.vector.tensor_copy(idxf[:, :], idx8[:, 0:2]))
                count(nc.vector.tensor_scalar(first[:, :], iota, idxf[:, 0:1], None, ALU.is_equal))

            def weigh_experts(p, k, t):
                low_bank = output_banks(k, t)[0]
                count, step = gate_counters(GATE_STEPS * (2 * p + t) + CHOOSE_STEPS)
                dve.wait_ge(sm["gate_exp"], 2 * p + t + 1)
                count(nc.vector.tensor_scalar(gs[:, 2:3], gs[:, 1:2], 1.0 / SCALING, 1.0 / SCALING, ALU.mult, ALU.add))
                step(nc.vector.tensor_scalar(second[:, :], iota, idxf[:, 1:2], gs[:, 1:2], ALU.is_equal, ALU.mult))
                count(nc.vector.reciprocal(gs[:, 3:4], gs[:, 2:3]))
                step(nc.vector.tensor_tensor(gates[:, :], first[:, :], second[:, :], ALU.add))
                nc.vector.scalar_tensor_tensor(out=gh[:, :].rearrange("p (e r) -> p e r", e=E2),
                                               in0=low_bank[:, 0:E2 * R2].rearrange("p (e r) -> p e r", e=E2),
                                               scalar=gs[:, 3:4], in1=gates[:, :].unsqueeze(2).broadcast_to([P, E2, R2]),
                                               op0=ALU.mult, op1=ALU.mult).then_inc(sm["gated"], 1)

            def gh_low(p, k, t):
                dve.wait_ge(sm["ghT_h"], 2 * p + t + 1)
                low(ghT_lo[:, :], gated_columns(k, t), ghT_hi[:, :], sm["ghT_l"])

            def finish(p, k, t):
                if k == 0 and t == 0:
                    dve.wait_ge(sm["bias_in"], 16)
                dve.wait_ge(sm["fin2"], 2 * p + t + 1)
                dve.wait_ge(stored[t], 16 * (p + 1))
                banks = output_banks(k, t)
                nc.vector.tensor_tensor(y[:, t, 0:OUT_A], banks[0][:, ROUT:HALF], bias_sb[:, 0:OUT_A],
                                        ALU.add).then_inc(sm["y_sb"], 1)
                nc.vector.tensor_tensor(y[:, t, OUT_A:D], banks[1][:, 0:HALF], bias_sb[:, OUT_A:D],
                                        ALU.add).then_inc(sm["y_sb"], 1)

            def full_weight(m):
                dve.wait_ge(sm["wprod"], m + 1)
                nc.vector.tensor_tensor(wfull[:, m, :], b_out[m % 2][:, :], wfull[:, m, :],
                                        ALU.add).then_inc(sm["wfull_sb"], 1)

            def full_low(m):
                dve.wait_ge(sm["wfull_h"], m + 1)
                low(wfull_lo[:, m, :], wfull[:, m, :], wfull_hi[:, m, :], sm["wfull_l"])

            def fused_weight(m):
                dve.wait_ge(sm["wprod"], C + m + 1)
                if m >= 2:
                    dve.wait_ge(sm["fused_l"], m - 1)
                nc.vector.tensor_copy(fused[:, m % 2, :], b_out[m % 2][:, :]).then_inc(sm["fused_sb"], 1)
                if m < C:
                    dve.wait_ge(sm["fused_sb"], 2 * m + 1)
                    block_m = fused[:, m % 2, P * m:P * m + P]
                    nc.vector.tensor_tensor(block_m, block_m, ident, ALU.add).then_inc(sm["fused_sb"], 1)

            def body(i, k):
                for s in range(SLOTS):
                    if s == 7 and pair(k - 1) and k < PAIRS - 1:
                        finish(i - 1, k - 1, 0)
                    if s == 7 and pair(k + 1):
                        rope_products(i + 1, k + 1, 1)
                    if s == 0 and pair(k - 1):
                        row_sums(i - 1, SLOTS - 1)
                    if s == 0 and k > 0 and pair(k + 1):
                        mix_low(i + 1, 1)
                    if s == 1 and pair(k - 2):
                        gh_low(i - 2, k - 2, 1)
                    if s == 6 and pair(k):
                        row_sums(i, s - 1)
                    if pair(k):
                        mask_and_max(i, k, s)
                    if s == 0 and pair(k):
                        k_low(i, 1)
                    if (k, s) == (0, 0):
                        mix_low(1, 1)
                    if s not in (0, 6) and pair(k):
                        row_sums(i, s - 1)
                    if s == 1 and pair(k - 1):
                        o_low(i - 1, 1)
                    if s == 2 and pair(k + 1):
                        rope_products(i + 1, k + 1, 0)
                    if s == 3 and k == -1:
                        mix_low(0, 1)
                        dve.wait_ge(sm["wf_in"], 16)
                        full_weight(0)
                    if s == 3 and pair(k - 1):
                        add_residual(i - 1, k - 1, 0)
                        if k == PAIRS - 1:
                            late_x1_low(i - 1, 0)
                    if s == 3 and pair(k + 1):
                        q_low(i + 1, 0)
                    if s == (3 if k < PAIRS - 1 else 5) and pair(k - 1):
                        add_residual(i - 1, k - 1, 1)
                        if k == PAIRS - 1:
                            late_x1_low(i - 1, 1)
                    if s == 6 and pair(k - 1) and k < PAIRS - 1:
                        gh_low(i - 1, k - 1, 0)
                    if s == 6 and pair(k):
                        o_low(i, 0)
                    if s == 1 and pair(k - 2):
                        finish(i - 2, k - 2, 1)
                    if s == (5 if k >= 0 else 4) and pair(k + 1):
                        k_low(i + 1, 0)
                    if s == (5 if k < PAIRS - 1 else 7) and pair(k - 1):
                        choose_experts(i - 1, k - 1, 0)
                        weigh_experts(i - 1, k - 1, 0)
                    if s == 7 and pair(k + 2):
                        mix_low(i + 2, 0)
                    if s == 7 and pair(k - 1) and k < PAIRS - 1:
                        choose_experts(i - 1, k - 1, 1)
                    if s == 7 and pair(k + 1):
                        q_low(i + 1, 1)
                    if s == 7 and pair(k - 1) and k < PAIRS - 1:
                        weigh_experts(i - 1, k - 1, 1)
                    if k == -1 and s == 0:
                        dve.wait_ge(sm["update_in"], 16 * 2)
                        nc.vector.tensor_tensor(cw[:, 2, :], cw[:, 0, :], cw[:, 1, :], ALU.mult).then_inc(sm["scaled"], 1)
                        dve.wait_ge(sm["scaled"], 1)
                        for e in range(2):
                            nc.vector.tensor_scalar(bf_sb[:, e, :], bf_sb[:, e, :], cw[:, 2, e:e + 1], None,
                                                    ALU.mult).then_inc(sm["scaled"], 1)
                    if (k, s) == (-1, 3):
                        full_weight(1)
                    if (k, s) == (-1, 7):
                        full_weight(2)
                        full_weight(3)
                    if (k, s) == (-1, 5):
                        full_low(0)
                        full_low(1)
                        for c in range(C // 2):
                            dve.wait_ge(sm["w2b2_h"], c + 1)
                            low(w2b2_lo[:, c, :], w2b2_raw[:, c, :], w2b2_hi[:, c, :], sm["w2b2_l"])
                    if (k, s) == (0, 0):
                        full_low(2)
                        full_low(3)
                    if k == 0 and s in FUSED_SLOTS:
                        fused_weight(FUSED_SLOTS.index(s))

            for c in range(C):
                dve.wait_ge(sm["wqkv_h"], c + 1)
                low(wqkv_lo[:, c, :], wqkv_raw[:, c, :], wqkv_hi[:, c, :], sm["wqkv_l"])
            steps(dve, body)
            p, q = PAIRS - 2, PAIRS - 1
            row_sums(q, 7)
            gh_low(p, p, 0)
            finish(p, p, 0)
            o_low(q, 1)
            choose_experts(p, p, 1)
            weigh_experts(p, p, 1)
            add_residual(q, q, 0)
            late_x1_low(q, 0)
            add_residual(q, q, 1)
            gh_low(p, p, 1)
            late_x1_low(q, 1)
            finish(p, p, 1)
            choose_experts(q, q, 0)
            weigh_experts(q, q, 0)
            choose_experts(q, q, 1)
            gh_low(q, q, 0)
            weigh_experts(q, q, 1)
            finish(q, q, 0)
            gh_low(q, q, 1)
            finish(q, q, 1)

        @block.tensor
        def _(pe):
            def split_product(dst, chunks, first=True, final=True):
                for c, (sh, sl, mh, ml) in enumerate(chunks):
                    for n, (a, b) in enumerate(((sh, mh), (sh, ml), (sl, mh))):
                        last = nc.tensor.matmul(dst, a, b, start=(first and c == 0 and n == 0),
                                                stop=(final and c == len(chunks) - 1 and n == 2))
                return last

            def mix(n, t):
                pe.wait_ge(x_in[t], 16 * (n + 1))
                pe.wait_ge(w_in[t], 64 * (n + 1))
                for c in range(C):
                    last = nc.tensor.matmul(b_mix[:, P * c:P * c + P], xt[:, t, P * c:P * c + P], wbd[:, t, :],
                                            start=True, stop=True)
                last.then_inc(sm["mixed"], 1)

            def project_q(n, k, t):
                pe.wait_ge(sm["hT_l"], 2 * n + t + 1)
                if k > 0 or t > 0:
                    pe.wait_ge(sm["qT_l"], 2 * n + t)
                for part in range(2):
                    if k == 0 and t == 0:
                        pe.wait_ge(sm["wqkv_l"], 2 * part + 2)
                    last = split_product(b_qkv[:, 0:D],
                                         [(hT_hi[:, t, c], hT_lo[:, t, c], wqkv_hi[:, c, 0:D], wqkv_lo[:, c, 0:D])
                                          for c in (2 * part, 2 * part + 1)], part == 0, part == 1)
                last.then_inc(sm["q_done"], 1)

            def project_kv(n, k, t):
                if k > 0 or t > 0:
                    pe.wait_ge(sm["kT_l"], 2 * n + t)
                split_product(b_qkv[:, D:QKV], [(hT_hi[:, t, c], hT_lo[:, t, c], wqkv_hi[:, c, D:QKV],
                                                 wqkv_lo[:, c, D:QKV]) for c in range(C)]).then_inc(sm["kv_done"], 1)

            def transpose_qk(n, t):
                pe.wait_ge(sm["roped"], 2 * n + t + 1)
                for r in range(REP):
                    last = nc.tensor.transpose(b_qkv[:, P * r:P * r + P], qk[:, r, :], ident)
                last.then_inc(sm["qT"], 1)
                pe.wait_ge(sm["v_out"], 2 * n + t + 1)
                nc.tensor.transpose(b_qkv[:, D:D + P], qk[:, REP, :], ident).then_inc(sm["kT"], 1)

            def scores(i, k, s):
                t, b = s // SEQ_PER_TILE, s % SEQ_PER_TILE
                if b == 0:
                    pe.wait_ge(sm["kbd_l"], 2 * (2 * i + t + 1))
                    pe.wait_ge(sm["qT_l"], 2 * i + t + 1)
                if k > 0 or s > 0:
                    pe.wait_ge(sm["masked"], 8 * i + s)
                keys = slice(S * b, S * b + S)
                split_product(b_s[:, 0:HKV * S], [(QT_hi[:, t, b].rearrange("p r s -> p (r s)"),
                                                   QT_lo[:, t, b].rearrange("p r s -> p (r s)"),
                                                   Kbd_hi[:, t, :, keys], Kbd_lo[:, t, :, keys])]
                              ).then_inc(sm["scored"], 1)

            def probs_T(i, k, s):
                pe.wait_ge(sm["normed"], 8 * i + s + 1)
                if k > 0 or s > 0:
                    pe.wait_ge(sm["pT_sb"], 8 * i + s)
                for h in range(2):
                    last = nc.tensor.transpose(b_pt[:, P * h:P * h + P],
                                               att[:, s % 4, 4 * h:4 * h + 4].rearrange("p g k -> p (g k)"), ident)
                last.then_inc(sm["pT"], 1)

            def values(i, k, s):
                t, b = s // SEQ_PER_TILE, s % SEQ_PER_TILE
                pe.wait_ge(sm["pT_sb"], 8 * i + s + 1)
                if b == 0:
                    pe.wait_ge(v_in[t], 64 * (i + 1))
                    if k > 0 or t > 0:
                        pe.wait_ge(sm["oT_l"], 2 * i + t)
                for h in range(2):
                    last = nc.tensor.matmul(b_o[64 * h:64 * h + 64, P * b:P * b + P], Vbd[:, t, b, h, :],
                                            PTs[:, s % 2, h, :], start=True, stop=True)
                last.then_inc(sm["pv"], 1)

            def output_projection(p, k, c):
                if c % 2 == 0 and 0 < k < PAIRS - 1:
                    pe.wait_ge(sm["y_sb"], 4 * p - 1 + c // 2)
                if c == 0:
                    if k == 0:
                        pe.wait_ge(sm["fused_sb"], 2 * C + 1)
                        pe.wait_ge(sm["wo_l"], C)
                    pe.wait_ge(sm["oT_l"], 2 * p + 2)
                o = [(wo_hi[:, r, P * c:P * c + P], wo_lo[:, r, P * c:P * c + P],
                      oT_hi[:, r].rearrange("p t b s -> p (t b s)"), oT_lo[:, r].rearrange("p t b s -> p (t b s)"))
                     for r in range(REP)]
                last = split_product(product_banks(k)[c // 2][:, 256 * (c % 2):256 * (c % 2) + 256], o)
                if c % 2:
                    last.then_inc(sm["wo_done"], 1)

            def output_layers(p, k, t, h):
                if t == 0 and h == 0:
                    pe.wait_ge(sm["x1_sum"], 2 * p + 2)
                    if k == 0:
                        pe.wait_ge(sm["fused_l"], C + 1)
                        pe.wait_ge(sm["a2r_l"], 1)
                if t == 1:
                    pe.wait_ge(sm["y_sb"], 4 * p + h + 1 if k < PAIRS - 1 else 4 * p - 1 + h)
                hi, lo = x1_parts(k)
                tok, cols = slice(P * t, P * t + P), slice(HALF * h, HALF * h + HALF)
                for part in range(2):
                    if t == 0 and h == 0:
                        pe.wait_ge(sm["x1_l"], 2 * p + part + 1)
                    last = split_product(output_banks(k, t)[h][:, 0:HALF],
                                         [(hi[:, c, tok], lo[:, c, tok], fw_hi[:, c, cols], fw_lo[:, c, cols])
                                          for c in (2 * part, 2 * part + 1)], part == 0, part == 1)
                if h == 0:
                    last.then_inc(sm["fin"], 1)

            def transpose_gated(p, k, t):
                pe.wait_ge(sm["gated"], 2 * p + t + 1)
                nc.tensor.transpose(gated_columns(k, t), gh[:, :], ident).then_inc(sm["ghT"], 1)

            def add_experts(p, k, t):
                banks = output_banks(k, t)
                pe.wait_ge(sm["ghT_l"], 2 * p + t + 1)
                for n, (a, b) in enumerate(((ghT_hi, bc_hi), (ghT_hi, bc_lo), (ghT_lo, bc_hi))):
                    nc.tensor.matmul(banks[0][:, ROUT:HALF], a[:, :], b[:, 0:OUT_A], start=False, stop=(n == 2),
                                     skip_group_check=True)
                    last = nc.tensor.matmul(banks[1][:, 0:HALF], a[:, :], b[:, OUT_A:D], start=False, stop=(n == 2),
                                            skip_group_check=True)
                last.then_inc(sm["fin2"], 1)

            def update_product(m):
                if m == 0:
                    pe.wait_ge(sm["update_in"], 16 * 2)
                    pe.wait_ge(sm["scaled"], 3)
                if m >= 2:
                    pe.wait_ge(sm["wfull_sb"], m - 1)
                for e in range(2):
                    last = nc.tensor.matmul(b_out[m % 2][:, :], af_sb[:, e, P * m:P * m + P], bf_sb[:, e, :],
                                            start=(e == 0), stop=(e == 1))
                last.then_inc(sm["wprod"], 1)

            def fused_product(m):
                if m == 0:
                    pe.wait_ge(sm["wfull_l"], C)
                    pe.wait_ge(sm["w2b2_l"], C)
                if m >= 2:
                    pe.wait_ge(sm["fused_sb"], 2 * (m - 2) + 1)
                cols = slice(P * m, P * m + P)
                last = split_product(b_out[m % 2][:, :], [(w2b2_hi[:, c, cols], w2b2_lo[:, c, cols], wfull_hi[:, c, :],
                                                           wfull_lo[:, c, :]) for c in range(C)])
                last.then_inc(sm["wprod"], 1)

            def body(i, k):
                a_next, a_after, w_now, w_tail = pair(k + 1), pair(k + 2), pair(k - 1), pair(k - 2)
                closing = k == PAIRS - 1
                for s in range(SLOTS):
                    if pair(k) and s != 1:
                        scores(i, k, s)
                    if s == 0 and closing:
                        output_layers(i - 2, k - 2, 1, 1)
                    late = pair(k - 1) if s < 2 else pair(k)
                    before = (i - 1, k - 1, SLOTS - 2 + s) if s < 2 else (i, k, s - 2)
                    if s == 6 and w_now and not closing:
                        if a_next:
                            pe.wait_ge(sm["v_out"], 2 * (i + 1) + 2)
                        transpose_gated(i - 1, k - 1, 0)
                    if late:
                        probs_T(*before)
                    if s == 0:
                        if a_next and k >= 0:
                            pe.wait_ge(sm["hT_l"], 2 * (i + 1) + 1)
                            mix(i + 1, 1)
                        if late:
                            values(*before)
                        if a_next:
                            project_q(i + 1, k + 1, 0)
                    if s == 1:
                        if w_tail:
                            if a_next:
                                pe.wait_ge(sm["hT_l"], 2 * (i + 1) + 2)
                            transpose_gated(i - 2, k - 2, 1)
                        if pair(k):
                            scores(i, k, s)
                        if late:
                            values(*before)
                        if a_next:
                            project_kv(i + 1, k + 1, 0)
                        if w_tail:
                            add_experts(i - 2, k - 2, 1)
                        if k == -1:
                            mix(0, 1)
                            update_product(0)
                        if k == 0:
                            fused_product(0)
                    if s == 2:
                        if w_now:
                            output_projection(i - 1, k - 1, 0)
                            output_projection(i - 1, k - 1, 1)
                        if k == 0:
                            fused_product(1)
                    if s == 3:
                        if w_now:
                            output_projection(i - 1, k - 1, 2)
                        if k == -1:
                            update_product(1)
                        if k == 0:
                            fused_product(2)
                        if a_next:
                            transpose_qk(i + 1, 0)
                        if w_now and not closing:
                            output_projection(i - 1, k - 1, 3)
                        if k == -1:
                            update_product(2)
                    if s == 4:
                        if a_next:
                            project_q(i + 1, k + 1, 1)
                        if closing:
                            output_projection(i - 1, k - 1, 3)
                    if s == 5:
                        if w_now and not closing:
                            output_layers(i - 1, k - 1, 0, 0)
                            output_layers(i - 1, k - 1, 0, 1)
                        if k == 0:
                            fused_product(3)
                        if a_next:
                            project_kv(i + 1, k + 1, 1)
                    if s == 6:
                        if a_after:
                            mix(i + 2, 0)
                        if closing:
                            output_layers(i - 1, k - 1, 0, 0)
                        elif w_now:
                            add_experts(i - 1, k - 1, 0)
                    if s == 7:
                        if pair(k):
                            values(i, k, SLOTS - 4)
                        if closing:
                            output_layers(i - 1, k - 1, 0, 1)
                        elif w_now:
                            output_layers(i - 1, k - 1, 1, 0)
                        if pair(k):
                            values(*before)
                        if w_now and k < PAIRS - 2:
                            output_layers(i - 1, k - 1, 1, 1)
                        if k == -1:
                            update_product(3)
                        if k == 0:
                            fused_product(4)
                        if a_next:
                            transpose_qk(i + 1, 1)
                    if late and s not in (0, 1, 6, 7):
                        values(*before)

            pe.wait_ge(sm["const_in"], 16)
            steps(pe, body)
            p, q = PAIRS - 2, PAIRS - 1
            probs_T(q, q, 6)
            transpose_gated(p, p, 0)
            values(q, q, 6)
            add_experts(p, p, 0)
            probs_T(q, q, 7)
            values(q, q, 7)
            output_layers(p, p, 1, 0)
            for c in range(C):
                output_projection(q, q, c)
            transpose_gated(p, p, 1)
            output_layers(p, p, 1, 1)
            add_experts(p, p, 1)
            output_layers(q, q, 0, 0)
            output_layers(q, q, 0, 1)
            output_layers(q, q, 1, 0)
            transpose_gated(q, q, 0)
            output_layers(q, q, 1, 1)
            add_experts(q, q, 0)
            transpose_gated(q, q, 1)
            add_experts(q, q, 1)


_OUT = (NSEQ, S, D)


def kernel(x, itok_B_0_15, itok_B_0_7, L0_cond_weights, L0_attn_Wq, L0_attn_Wk, L0_attn_Wv, L0_attn_Wo,
           L0_cond2_W, L0_cond2_Wr, L0_cond2_A, L0_cond2_B, L0_ffn_W, L0_ffn_bias, L0_ffn_A, L0_ffn_Bf,
           L0_ffn_coeffs, L0_ffn_scales):
    import concourse.bacc as _bacc
    from concourse.bass_utils import run_bass_kernel_spmd as _run

    def chunked(w, n=C):
        return np.ascontiguousarray(np.asarray(w).reshape(n, P, -1).transpose(1, 0, 2))

    x = np.ascontiguousarray(x)
    q_rows = np.asarray(L0_attn_Wq).reshape(HKV, REP, HD, D).transpose(1, 0, 2, 3).reshape(D, D)
    qkv_rows = np.concatenate([q_rows, np.asarray(L0_attn_Wk), np.asarray(L0_attn_Wv)], 0)
    o_cols = np.asarray(L0_attn_Wo).reshape(D, HKV, REP, HD).transpose(2, 1, 3, 0).reshape(D, D)
    a2 = np.asarray(L0_cond2_A).reshape(E2 * R2, D)
    a2r = np.concatenate([a2, np.asarray(L0_cond2_Wr)], 0).T
    b2 = np.asarray(L0_cond2_B).transpose(1, 0, 2).reshape(D, E2 * R2)
    bf = np.asarray(L0_ffn_Bf).transpose(0, 2, 1).reshape(EF * 16, D)
    lang = np.asarray(itok_B_0_7).reshape(PAIRS, 2, SEQ_PER_TILE, 1)
    lang = np.broadcast_to(lang, (PAIRS, 2, SEQ_PER_TILE, S)).reshape(PAIRS, 2, P).transpose(0, 2, 1)

    inv = (1.0 / 10000.0 ** (np.arange(0, HD, 2, dtype=np.float32) / np.float32(HD))).astype(np.float32)
    ang = np.outer(np.arange(S, dtype=np.float32), inv)
    c, s_ = np.cos(ang), np.sin(ang)
    consts = np.zeros((P, K_ALL), np.float32)
    consts[:, K_COS:K_COS + HD] = np.tile(np.concatenate([c, c], 1), (SEQ_PER_TILE, 1))
    consts[:, K_SIN:K_SIN + HD] = np.tile(np.concatenate([-s_, s_], 1), (SEQ_PER_TILE, 1))
    consts[:, K_MASK:K_MASK + S] = np.tile(np.triu(np.full((S, S), MASKED, np.float32), 1), (REP, 1))
    consts[:, K_IOTA:K_IOTA + E2] = np.arange(E2)
    consts[:, K_GROUP:K_GROUP + HKV] = np.repeat(np.eye(HKV), HD, 0)
    consts[:, K_ID:K_ID + P] = np.eye(P)

    given = {
        "x": x,
        "xT": np.ascontiguousarray(x.reshape(NSEQ * S, D).T),
        "cond": np.ascontiguousarray(itok_B_0_15),
        "lang": np.ascontiguousarray(lang),
        "wcond": np.ascontiguousarray(L0_cond_weights),
        "wqkv": chunked(qkv_rows.T),
        "wo": chunked(o_cols),
        "w2b2": chunked(np.concatenate([np.asarray(L0_cond2_W), b2], 1)),
        "a2r": chunked(a2r),
        "wf": chunked(np.asarray(L0_ffn_W).T),
        "afbf": chunked(np.concatenate([np.asarray(L0_ffn_A).reshape(EF * 16, D), bf], 0), 4),
        "cs": np.ascontiguousarray(np.stack([np.repeat(np.asarray(v), 16).reshape(2, P)
                                             for v in (L0_ffn_coeffs, L0_ffn_scales)]).transpose(2, 0, 1)),
        "bias": np.ascontiguousarray(L0_ffn_bias),
        "consts": consts,
    }
    nc = _bacc.Bacc("TRN2", target_bir_lowering=False, num_devices=1)
    arrays, args = {}, {}
    for name, a in given.items():
        arrays[f"{name}_dram"] = a
        args[name] = nc.dram_tensor(f"{name}_dram", a.shape, mybir.dt.from_np(a.dtype), kind="ExternalInput").ap()
    out = nc.dram_tensor("out_dram", _OUT, F32, kind="ExternalOutput").ap()
    program(nc, out=out, **args)
    r = _run(nc, [arrays], core_ids=[0])
    return r.results[0]["out_dram"]
```
